# Optimizing a Trainium2 kernel written in Bass

```python
import numpy as np
import jax
import jax.numpy as jnp

def _softmax(x, axis=-1):
    return jax.nn.softmax(x, axis=axis)

def _gelu(x):
    return jax.nn.gelu(x, approximate=True)

def _silu(x):
    return jax.nn.silu(x)

def _sigmoid(x):
    return jax.nn.sigmoid(x)

def _layernorm(x, axis=-1, eps=1e-05):
    m = jnp.mean(x, axis=axis, keepdims=True)
    v = jnp.var(x, axis=axis, keepdims=True)
    return (x - m) / jnp.sqrt(v + eps)

def _scatter_add(tgt, idx, src, axis=0):
    return tgt.at[idx].add(src)

def _segment_sum(src, seg, n):
    return jax.ops.segment_sum(src, seg, n)
kernel_name = 'mk_flamingo_gated_d1_seqx_r4_d4e787'

def setup_inputs(seed: int=0):
    np.random.seed(seed)
    _w = jnp.asarray

    def _rec_inputs():
        import jax
        import jax.numpy as jnp
        _rk = jax.random.key(seed)
        x = 7.22e-05 + 1 * jax.random.normal(jax.random.fold_in(_rk, 1), (4, 512, 512), jnp.float32)
        _lenS = 512 - jax.random.randint(jax.random.fold_in(_rk, 7), (4,), 0, max(1, 512 // 4) + 1, jnp.int32)
        _lenS2 = 64 - jax.random.randint(jax.random.fold_in(_rk, 8), (4,), 0, max(1, 64 // 4) + 1, jnp.int32)
        _ctx_512P = jax.random.normal(jax.random.fold_in(_rk, 11), (4, 16, 128), jnp.float32)
        _ctx_512c = jax.random.dirichlet(jax.random.fold_in(_rk, 511), 0.3 * jnp.ones((16,), jnp.float32), (4, 64))
        _ctx_512t = jnp.einsum('bsk,bkd->bsd', _ctx_512c, _ctx_512P)
        _ctx_512t = _ctx_512t * jax.lax.rsqrt(jnp.mean(jnp.square(_ctx_512t)) + 1e-12) * 0.953939
        ctx_512 = -0.000514642 + 1.00011 * (_ctx_512t + 0.3 * jax.random.normal(jax.random.fold_in(_rk, 611), (4, 64, 128), jnp.float32))
        _g = jax.random.normal(jax.random.fold_in(_rk, 9001), (2, 1), jnp.float32)
        _g = jnp.sign(_g) * jnp.maximum(jnp.abs(_g), 1.0) + (_g == 0) * 1.0
        g_xattn = _g[0]
        g_ffn = _g[1]
        return (x, ctx_512, g_xattn, g_ffn)
    x, ctx_512, g_xattn, g_ffn = _rec_inputs()

    def _L0_xattn_setup():
        import jax, jax.numpy as jnp
        import numpy as np
        B, S, H, NH, L = (2, 512, 512, 16, 128)
        HD = H // NH
        key = jax.random.key(seed)
        k1, k2, k3, k4, k5 = jax.random.split(key, 5)
        scale = 0.02
        return {'q': jax.random.normal(k1, (B, S, H), dtype=jnp.float32), 'latent_kv': jax.random.normal(k2, (B, S, L), dtype=jnp.float32), 'Wq': jax.random.normal(k3, (H, H), dtype=jnp.float32) * scale, 'Wkv_expand': jax.random.normal(k4, (2 * H, L), dtype=jnp.float32) * scale, 'Wout': jax.random.normal(k5, (H, H), dtype=jnp.float32) * scale}
    _L0_xattn_all = _L0_xattn_setup()
    _L0_xattn_in = {k: v for k, v in _L0_xattn_all.items() if k in ('Wq', 'Wkv_expand', 'Wout')}
    del _L0_xattn_all

    def _L0_ffn_setup():
        import jax, jax.numpy as jnp
        import numpy as np
        B, S, DIM = (2, 512, 512)
        INTER = 256
        E = 8
        K = 2
        N_SHARED = 1
        ROUTE_SCALE = 1.0
        key = jax.random.key(seed)
        ks = jax.random.split(key, 8)
        s_in = 1.0 / np.sqrt(DIM)
        s_hid = 1.0 / np.sqrt(INTER)
        return {'x': jax.random.normal(ks[0], (B, S, DIM), dtype=jnp.float32), 'gate_w': jax.random.normal(ks[1], (E, DIM), dtype=jnp.float32) * s_in, 'w1': jax.random.normal(ks[2], (E, INTER, DIM), dtype=jnp.float32) * s_in, 'w2': jax.random.normal(ks[3], (E, DIM, INTER), dtype=jnp.float32) * s_hid, 'w3': jax.random.normal(ks[4], (E, INTER, DIM), dtype=jnp.float32) * s_in, 'ws1': jax.random.normal(ks[5], (N_SHARED * INTER, DIM), dtype=jnp.float32) * s_in, 'ws2': jax.random.normal(ks[6], (DIM, N_SHARED * INTER), dtype=jnp.float32) * s_hid, 'ws3': jax.random.normal(ks[7], (N_SHARED * INTER, DIM), dtype=jnp.float32) * s_in}
    _L0_ffn_all = _L0_ffn_setup()
    _L0_ffn_in = {k: v for k, v in _L0_ffn_all.items() if k in ('gate_w', 'w1', 'w2', 'w3', 'ws1', 'ws2', 'ws3')}
    del _L0_ffn_all
    return {'x': x, 'ctx_512': ctx_512, 'g_xattn': g_xattn, 'g_ffn': g_ffn, 'L0_xattn_Wq': _L0_xattn_in['Wq'], 'L0_xattn_Wkv_expand': _L0_xattn_in['Wkv_expand'], 'L0_xattn_Wout': _L0_xattn_in['Wout'], 'L0_ffn_gate_w': _L0_ffn_in['gate_w'], 'L0_ffn_w1': _L0_ffn_in['w1'], 'L0_ffn_w2': _L0_ffn_in['w2'], 'L0_ffn_w3': _L0_ffn_in['w3'], 'L0_ffn_ws1': _L0_ffn_in['ws1'], 'L0_ffn_ws2': _L0_ffn_in['ws2'], 'L0_ffn_ws3': _L0_ffn_in['ws3']}

def reference(x, ctx_512, g_xattn, g_ffn, L0_xattn_Wq, L0_xattn_Wkv_expand, L0_xattn_Wout, L0_ffn_gate_w, L0_ffn_w1, L0_ffn_w2, L0_ffn_w3, L0_ffn_ws1, L0_ffn_ws2, L0_ffn_ws3):
    import jax
    import jax.numpy as jnp

    def _L0_xattn_ref(q, latent_kv, Wq, Wkv_expand, Wout):
        import jax, jax.numpy as jnp
        import numpy as np
        B, S, H, NH, L = (2, 512, 512, 16, 128)
        HD = H // NH
        b, sq, _ = q.shape
        sk = latent_kv.shape[1]
        qp = q @ Wq.T
        kv = latent_kv @ Wkv_expand.T
        k, v = jnp.split(kv, 2, axis=-1)
        qh = qp.reshape(b, sq, NH, HD).transpose(0, 2, 1, 3)
        kh = k.reshape(b, sk, NH, HD).transpose(0, 2, 1, 3)
        vh = v.reshape(b, sk, NH, HD).transpose(0, 2, 1, 3)
        inv_sqrt_d = 1.0 / jnp.sqrt(jnp.float32(HD))
        scores = jnp.einsum('bhqd,bhkd->bhqk', qh, kh) * inv_sqrt_d
        causal = jnp.tril(jnp.ones((sq, sk), dtype=bool))
        scores = jnp.where(causal, scores, jnp.finfo(scores.dtype).min)
        attn = jax.nn.softmax(scores, axis=-1)
        out = jnp.einsum('bhqk,bhkd->bhqd', attn, vh)
        out = out.transpose(0, 2, 1, 3).reshape(b, sq, H)
        return out @ Wout.T

    def _L0_ffn_ref(x, gate_w, w1, w2, w3, ws1, ws2, ws3):
        import jax, jax.numpy as jnp
        import numpy as np
        B, S, DIM = (2, 512, 512)
        INTER = 256
        E = 8
        K = 2
        N_SHARED = 1
        ROUTE_SCALE = 1.0
        shape = x.shape
        xf = x.reshape(-1, DIM)
        scores = jax.nn.softmax(xf @ gate_w.T, axis=-1)
        weights, idx = jax.lax.top_k(scores, K)
        weights = weights * ROUTE_SCALE
        h = jnp.einsum('td,eid->eti', xf, w1)
        g = jax.nn.silu(h) * jnp.einsum('td,eid->eti', xf, w3)
        eo = jnp.einsum('eti,edi->etd', g, w2)
        comb = jnp.einsum('tke,tk->te', jax.nn.one_hot(idx, E, dtype=xf.dtype), weights)
        y = jnp.einsum('etd,te->td', eo, comb)
        z = jax.nn.silu(xf @ ws1.T) * (xf @ ws3.T) @ ws2.T
        return (y + z).reshape(shape)
    x = x + jnp.tanh(g_xattn[0]) * _L0_xattn_ref(_layernorm(x, axis=-1), ctx_512, L0_xattn_Wq, L0_xattn_Wkv_expand, L0_xattn_Wout)
    x = x + jnp.tanh(g_ffn[0]) * _L0_ffn_ref(_layernorm(x, axis=-1), L0_ffn_gate_w, L0_ffn_w1, L0_ffn_w2, L0_ffn_w3, L0_ffn_ws1, L0_ffn_ws2, L0_ffn_ws3)
    return x

_drawn_inputs = setup_inputs


def setup_inputs(seed=0):
    import zlib

    import numpy as np

    out = dict(_drawn_inputs(seed))
    spreads = {}
    factors = {'L0_xattn_Wq': 8.0}
    for name, (base, spread) in spreads.items():
        noise = np.random.default_rng([zlib.crc32(name.encode()), seed]).standard_normal(out[name].shape)
        drawn = base * np.exp(spread * noise) if base else spread * noise
        out[name] = jnp.asarray(drawn.astype(out[name].dtype))
    for name, factor in factors.items():
        out[name] = (out[name] * factor).astype(out[name].dtype)
    return out
```

```python
from contextlib import ExitStack

import numpy as np
import concourse.bass as bass
import concourse.mybir as mybir

F32 = mybir.dt.float32
F16 = mybir.dt.float16
I32 = mybir.dt.int32
ALU = mybir.AluOpType
ACT = mybir.ActivationFunctionType
AX = mybir.AxisListType
PE_ENGINE = mybir.EngineType.PE
SP_ENGINE = mybir.EngineType.SP

P = 128
B, SQ, D = 4, 512, 512
SK, L = 64, 128
NH, HD = 16, 32
E, INTER = 8, 256
TOK = B * SQ
NT = TOK // P
PER = SQ // P
DC = D // P
IC = INTER // P
GH = P // HD
NG = NH // GH
PR = NH // 2
EPS = 1e-5

LIST = TOK
TILES = 2 * TOK // P + E - 1
LISTS = E * LIST + E * P
ROWS = TOK + P
RING = 3
ROUNDS = TILES // RING
assert ROUNDS * RING == TILES

S_LN = 16.0
S_W = 256.0
S_CTX = 16.0
S_Q = 16.0
S_KV = 128.0
S_P = 1024.0
S_A = 128.0
S_G = 16.0
FILL = -3.0e38
WE = 2 * (DC + IC) * D
HALF = WE // 2


def block_program(nc, x, ctx_rows, gates, wq, wkv, wout, gate_w, experts, out):
    with ExitStack() as stack:
        def sb(name, shape, dt=F32):
            return stack.enter_context(nc.sbuf_tensor(name, shape, dt))

        def sem(name):
            return stack.enter_context(nc.semaphore(name))

        xrows = nc.dram_tensor("xrows", (ROWS, D), F32)
        lists = nc.dram_tensor("lists", (LISTS, 2), I32)

        arena = sb("arena", [P, (E + 1) * WE // 2])
        arena16 = arena[:, :].bitcast(F16)
        taken = [0]

        def part(n, dt=F32):
            at = taken[0]
            taken[0] = at + n
            assert taken[0] <= E * WE // 2
            v = arena[:, at:at + n]
            return v if dt == F32 else v.bitcast(dt)

        S = part(PER * NH * SK)
        PT = part(PR * SQ, F16)
        xT = part(DC * SQ, F16)
        xn1 = part(PER * D)
        qT = part(NG * SQ, F16)
        aT = part(NG * SQ, F16)
        wq_s = part(DC * D, F16)
        wout_s = part(DC * D, F16)
        kc = part(NG * B * SK, F16).rearrange("p (h g b k) -> p h g b k", h=2, g=NG, b=B)
        kbd = part(NG * GH * SK, F16)
        vc = part(B * D, F16).rearrange("p (h b n) -> p h b n", h=2, b=B)
        vbd = sb("vbd", [P, 2 * PR * P], F16)
        PTv = PT.rearrange("p (h r t) -> p h r t", h=2, r=PR)
        xTv = xT.rearrange("p (h c t) -> p h c t", h=2, c=DC)
        qTv = qT.rearrange("p (h g t) -> p h g t", h=2, g=NG)
        aTv = aT.rearrange("p (h g t) -> p h g t", h=2, g=NG)
        wqv = wq_s.rearrange("p (h c n) -> p h c n", h=2, c=DC)
        woutv = wout_s.rearrange("p (h c n) -> p h c n", h=2, c=DC)
        kbdv = kbd.rearrange("p (h g m) -> p h g m", h=2, g=NG)
        vbdv = vbd[:, :].rearrange("p (h r m) -> p h r m", h=2, r=PR)
        wq_raw = S[:, 0:DC * D]
        wout_raw = S[:, DC * D:2 * DC * D]
        wkv_raw = PT[:, 0:4 * D].bitcast(F32)
        ctx_raw = PT[:, 4 * D:4 * D + 4 * B * SK].bitcast(F32)

        wkv_s = sb("wkv_s", [P, 2, 2 * D], F16)
        ctx_s = sb("ctx_s", [P, 2, B, 2, SK], F16)
        gate_raw = sb("gate_raw", [P, DC * E])
        gate_s = sb("gate_s", [P, 2, DC, E], F16)
        x_sb = sb("x_sb", [P, NT * D])
        xn2 = sb("xn2", [P, PER * D])
        x2T = sb("x2T", [P, 2, DC, SQ], F16)
        th = sb("th", [P, RING, INTER])
        uu = sb("uu", [P, RING, INTER])
        gg = sb("gg", [P, RING, INTER])
        gT = sb("gT", [P, 2, IC, P], F16)
        G = sb("G", [P, RING, D])
        GT = sb("GT", [P, RING, 2, DC, P], F16)
        shared_raw = [G[:, :, :].rearrange("p s d -> p (s d)"),
                      GT[:, :, :, :, :].rearrange("p s h c t -> p (s h c t)").bitcast(F32)]
        Y = sb("Y", [P, RING, D])
        fresh = sb("fresh", [P, RING, 2], I32)
        entry = sb("entry", [P, RING, 2], I32)
        ident = sb("ident", [P, P])
        earlier = sb("earlier", [P, P], F16)
        ones16 = sb("ones16", [P, P], F16)
        mv = sb("mv", [P, 2, PER, 8])
        ln = sb("ln", [P, 2, PER, 4])
        minus_half = sb("minus_half", [P, PER])
        mx = sb("mx", [P, PER, NH])
        rd = sb("rd", [P, PER, NH])
        gl = sb("gl", [P, 4])
        lg = sb("lg", [P, PER, E])
        ex = sb("ex", [P, PER, E])
        sc = sb("sc", [P, PER, E])
        sc2 = sb("sc2", [P, PER, E])
        eq = sb("eq", [P, PER, E])
        oh = sb("oh", [P, 2, PER, E])
        pos = sb("pos", [P, PER, E])
        sel = sb("sel", [P, PER, E])
        m = sb("m", [P, 6, PER])
        mask16 = sb("mask16", [P, PER * E], F16)
        first_high = sb("first_high", [P, E])
        list_at = sb("list_at", [P, E])
        seen = sb("seen", [P, E])
        slot = sb("slot", [P, PER, 2], I32)
        pair = sb("pair", [P, PER, 2, 2], I32)
        empty = sb("empty", [P, LISTS // P, 2], I32)
        count = sb("count", [P, 6, E])
        count_i = sb("count_i", [P, 2, E], I32)
        tile_no = sb("tile_no", [P, TILES])
        past = sb("past", [P, TILES, E])
        skip = sb("skip", [P, TILES, E])
        tab_f = sb("tab_f", [P, 2, TILES])
        tab = sb("tab", [P, 2, TILES], I32)

        bank = [stack.enter_context(nc.psum_tensor(f"bank{n}", [P, 512], F32)) for n in range(8)]
        score_bank, turn_bank, mm_bank = bank[0:2], bank[2:4], bank[4:8]
        e_turn, e_h, e_g, e_y = bank[0], bank[1:4], bank[4], bank[5:8]

        ld_gates, ld_kv, ld_x0, ld_x, ld_wq, ld_wout, ld_gate = (sem(n) for n in (
            "ld_gates", "ld_kv", "ld_x0", "ld_x", "ld_wq", "ld_wout", "ld_gate"))
        ld_shared = sem("ld_shared")
        ld_w = [sem(f"ld_w{n}") for n in range(4)]
        passed = sem("passed")
        consts = sem("consts")
        zeroed = sem("zeroed")
        tanh_gates, gates_ready = sem("tanh_gates"), sem("gates_ready")
        kv_hi, kv_lo = sem("kv_hi"), sem("kv_lo")
        wq_hi, wq_lo, wout_hi, wout_lo = sem("wq_hi"), sem("wq_lo"), sem("wout_hi"), sem("wout_lo")
        gate_hi, gate_lo, shared_hi, shared_lo = (sem(n) for n in ("gate_hi", "gate_lo", "shared_hi", "shared_lo"))
        k_mm, k_hi, k_lo, v_mm, v_hi, v_lo = (sem(n) for n in ("k_mm", "k_hi", "k_lo", "v_mm", "v_hi", "v_lo"))
        k_filled, v_filled = sem("k_filled"), sem("v_filled")
        ln1_step, ln1_stats, xn1_ready = sem("ln1_step"), sem("ln1_stats"), sem("xn1_ready")
        ln1_var, ln1_power, ln2_var, ln2_power = (sem(n) for n in ("ln1_var", "ln1_power", "ln2_var", "ln2_power"))
        xT_mm, xT_hi, xT_lo = sem("xT_mm"), sem("xT_hi"), sem("xT_lo")
        q_mm, q_hi, q_lo = sem("q_mm"), sem("q_hi"), sem("q_lo")
        s_mm, s_copied, masked, max_ready, sub_ready, exp_ready, sum_ready, rd_ready, p_ready = (sem(n) for n in (
            "s_mm", "s_copied", "masked", "max_ready", "sub_ready", "exp_ready", "sum_ready", "rd_ready", "p_ready"))
        pT_mm, pT_hi, pT_lo = sem("pT_mm"), sem("pT_hi"), sem("pT_lo")
        a_mm, a_hi, a_lo = sem("a_mm"), sem("a_hi"), sem("a_lo")
        y_mm, x1_ready = sem("y_mm"), sem("x1_ready")
        ln2_step, ln2_stats, xn2_ready = sem("ln2_step"), sem("ln2_stats"), sem("xn2_ready")
        x2T_mm, x2T_hi, x2T_lo = sem("x2T_mm"), sem("x2T_hi"), sem("x2T_lo")
        lg_mm, lg_max, lg_out, lg_exp = sem("lg_mm"), sem("lg_max"), sem("lg_out"), sem("lg_exp")
        route_step, mask_ready, pos_mm, route2_step, pos_out, pairs_ready = (sem(n) for n in (
            "route_step", "mask_ready", "pos_mm", "route2_step", "pos_out", "pairs_ready"))
        h_mm, th_ready, u_ready, g_ready = sem("h_mm"), sem("th_ready"), sem("u_ready"), sem("g_ready")
        gT_mm, gT_hi, gT_lo = sem("gT_mm"), sem("gT_hi"), sem("gT_lo")
        z_mm, base_ready = sem("z_mm"), sem("base_ready")
        st_rows, st_base, st_pairs, st_init = sem("st_rows"), sem("st_base"), sem("st_pairs"), sem("st_init")
        w_hi, w_lo = sem("w_hi"), sem("w_lo")
        table_step, table_ready = sem("table_step"), sem("table_ready")
        ld_list = [sem(f"ld_list{n}") for n in range(RING)]
        ld_rows = [sem(f"ld_rows{n}") for n in range(RING)]
        added = [sem(f"added{n}") for n in range(RING)]
        eT_mm, eT_hi, eT_lo = sem("eT_mm"), sem("eT_hi"), sem("eT_lo")
        eh_mm, eth_ready, eu_ready, eg_ready = sem("eh_mm"), sem("eth_ready"), sem("eu_ready"), sem("eg_ready")
        egT_mm, egT_hi, egT_lo = sem("egT_mm"), sem("egT_hi"), sem("egT_lo")
        ey_mm, ey_ready, entry_ready = sem("ey_mm"), sem("ey_ready"), sem("entry_ready")

        def x_tile(t):
            return x_sb[:, bass.ds(t * D, D)]

        def w_piece(k):
            e, h = divmod(k, 2)
            at = e * WE + h * (HALF // 2)
            raw = x_sb[:, (k % 4) * (HALF // 2):(k % 4 + 1) * (HALF // 2)]
            return raw, arena16[:, at:at + HALF // 2], arena16[:, at + HALF:at + HALF + HALF // 2]

        PIECES = 2 * E
        CONSTS = 15

        def pass_waits(eng):
            eng.sem_inc(passed, 1)

        stack.enter_context(nc.allow_low_precision(reason="sums of whole numbers below 2^24, written as int32"))
        block = stack.enter_context(nc.Block())

        @block.sync
        def _(sp):
            sp.dma_start(ctx_raw.rearrange("p (b e k) -> p b e k", b=B, e=2), ctx_rows).then_inc(ld_kv, 16)
            sp.dma_start(wkv_raw, wkv).then_inc(ld_kv, 16)
            sp.dma_start(x_sb[:, 0:PER * D].rearrange("p (t d) -> p t d", t=PER), x[:, 0:PER, :]).then_inc(ld_x0, 16)
            sp.dma_start(gl[:, 0:2], gates).then_inc(ld_gates, 16)
            sp.dma_start(wq_raw, wq).then_inc(ld_wq, 16)
            sp.dma_start(gate_raw[:, :], gate_w).then_inc(ld_gate, 16)
            sp.dma_start(wout_raw, wout).then_inc(ld_wout, 16)
            sp.dma_start(x_sb[:, PER * D:NT * D].rearrange("p (t d) -> p t d", t=NT - PER),
                         x[:, PER:NT, :]).then_inc(ld_x, 16)
            for h in range(2):
                sp.dma_start(shared_raw[h], experts[E][:, h * (HALF // 2):(h + 1) * (HALF // 2)]).then_inc(ld_shared, 16)
            sp.wait_ge(zeroed, 1)
            sp.dma_start(xrows[TOK:ROWS, :], Y[:, 0, :]).then_inc(st_init, 16)
            sp.dma_start(out[TOK:ROWS, :], Y[:, 0, :]).then_inc(st_init, 16)
            sp.wait_ge(zeroed, 2)
            sp.dma_start(lists[:, :].rearrange("(p f) c -> p (f c)", p=P),
                         empty[:, :, :].rearrange("p f c -> p (f c)")).then_inc(st_init, 16)

            def store_base(b):
                for i in range(PER):
                    sp.wait_ge(base_ready, 4 * b + i + 1)
                    sp.dma_start(out[bass.ds((4 * b + i) * P, P), :], x_tile(4 * b + i)).then_inc(st_base, 16)

            def store_rows(b):
                for i in range(PER):
                    sp.wait_ge(xn2_ready, 4 * b + i + 1)
                    sp.dma_start(xrows[bass.ds((4 * b + i) * P, P), :],
                                 xn2[:, i * D:(i + 1) * D]).then_inc(st_rows, 16)

            store_rows(0)
            with sp.Fori(1, B - 1) as b:
                store_base(b - 1)
                store_rows(b)
            store_base(B - 2)
            sp.wait_ge(st_base, 16 * PER * (B - 1))
            for k in range(4):
                sp.dma_start(w_piece(k)[0], experts[k // 2][:, (k % 2) * (HALF // 2):(k % 2 + 1) * (HALF // 2)]
                             ).then_inc(ld_w[k], 16)
            store_rows(B - 1)

            def later_pieces(lo, hi):
                for k in range(lo, hi):
                    sp.wait_ge(w_lo, k - 3)
                    sp.dma_start(w_piece(k)[0], experts[k // 2][:, (k % 2) * (HALF // 2):(k % 2 + 1) * (HALF // 2)]
                                 ).then_inc(ld_w[k % 4], 16)

            later_pieces(4, 8)
            for i in range(PER):
                sp.wait_ge(base_ready, 4 * (B - 1) + i + 1)
                sp.dma_start(out[(4 * (B - 1) + i) * P:(4 * (B - 1) + i + 1) * P, :],
                             x_tile(4 * (B - 1) + i)).then_inc(st_base, 16)
            later_pieces(8, PIECES)

            sp.wait_ge(table_ready, 1)
            sp.wait_ge(st_init, 48)
            sp.wait_ge(st_pairs, 16 * 2 * NT)

            def load_list(j, s):
                at = nc.values_load(tab[0:1, 1, bass.ds(j, 1)], engines=[SP_ENGINE], min_val=0, max_val=LISTS - P,
                                    skip_runtime_bounds_check_because="tiles end within the lists and their spare part")
                sp.dma_start(fresh[:, s, :], lists[bass.ds(at, P), :]).then_inc(ld_list[s], 16)

            for s in range(RING):
                load_list(s, s)

            def list_step(it, s):
                j = RING * it + s
                sp.wait_ge(entry_ready, j + 1)
                sp.wait_ge(ld_rows[s], 16 * (it + 1))
                load_list(j + RING, s)

            for s in range(RING):
                list_step(0, s)
            with sp.Fori(1, ROUNDS - 1) as it:
                for s in range(RING):
                    list_step(it, s)

        @block.gpsimd
        def _(pool):
            pool.memset(ident[:, :], 0.0).then_inc(consts, 1)
            pool.memset(earlier[:, :], 1.0).then_inc(consts, 1)
            pool.memset(ones16[:, :], 1.0).then_inc(consts, 1)
            pool.wait_ge(consts, 3)
            pool.affine_select(out=ident[:, :], in_=ident[:, :], compare_op=ALU.not_equal, fill=1.0,
                               base=0, pattern=[[-1, P]], channel_multiplier=1).then_inc(consts, 1)
            pool.affine_select(out=earlier[:, :], in_=earlier[:, :], compare_op=ALU.is_gt, fill=0.0,
                               base=0, pattern=[[1, P]], channel_multiplier=-1).then_inc(consts, 1)
            pool.memset(kbd.bitcast(F32), 0.0).then_inc(consts, 1)
            pool.memset(vbd[:, :].bitcast(F32), 0.0).then_inc(consts, 1)
            pool.iota(first_high[:, :], pattern=[[-1, E]], base=E, channel_multiplier=0,
                      allow_small_or_imprecise_dtypes=True).then_inc(consts, 1)
            pool.iota(list_at[:, :], pattern=[[LIST, E]], base=0, channel_multiplier=0,
                      allow_small_or_imprecise_dtypes=True).then_inc(consts, 1)
            pool.iota(seen[:, :], pattern=[[LIST, E]], base=0, channel_multiplier=0,
                      allow_small_or_imprecise_dtypes=True).then_inc(consts, 1)
            pool.iota(pair[:, :, :, 0], pattern=[[P, PER], [0, 2]], base=-SQ, channel_multiplier=1).then_inc(consts, 1)
            pool.iota(tile_no[:, :], pattern=[[1, TILES]], base=0, channel_multiplier=0,
                      allow_small_or_imprecise_dtypes=True).then_inc(consts, 1)
            pool.memset(minus_half[:, :], -0.5).then_inc(consts, 1)
            pool.memset(Y[:, 0, :], 0.0).then_inc(zeroed, 1)
            pool.iota(empty[:, :, 0], pattern=[[1, LISTS // P]], base=0,
                      channel_multiplier=LISTS // P).then_inc(consts, 1)
            pool.memset(empty[:, :, 1], 0).then_inc(consts, 1)

            def power(b, which, var, done):
                pool.wait_ge(var, b + 1)
                nc.gpsimd.tensor_tensor(ln[:, which, :, 2], ln[:, which, :, 1], minus_half[:, :],
                                        ALU.pow).then_inc(done, 1)

            pool.wait_ge(consts, CONSTS)
            power(0, 0, ln1_var, ln1_power)
            def scatter_pairs(b):
                pool.wait_ge(st_init, 48)
                pool.wait_ge(pairs_ready, b + 1)
                pass_waits(pool)
                for i in range(PER):
                    for k in range(2):
                        nc.gpsimd.indirect_dma_start(
                            out=lists[:, :], out_offset=bass.IndirectOffsetOnAxis(ap=slot[:, i, k:k + 1], axis=0),
                            in_=pair[:, i, k, :], in_offset=None).then_inc(st_pairs, 16)

            def softmax_sub(b, i):
                t = 4 * b + i
                si = S[:, i * NH * SK:(i + 1) * NH * SK]
                sv = si.rearrange("p (h k) -> p h k", h=NH)
                if i == 0:
                    pool.wait_ge(s_copied, 2 * t + 2)
                    pass_waits(pool)
                    pool.affine_select(out=sv, in_=sv, compare_op=ALU.is_ge, fill=FILL, base=0,
                                       pattern=[[0, NH], [-1, SK]], channel_multiplier=1).then_inc(masked, 1)
                pool.wait_ge(max_ready, t + 1)
                nc.gpsimd.tensor_tensor(sv, sv, mx[:, i, :].unsqueeze(2).to_broadcast([P, NH, SK]),
                                        ALU.subtract).then_inc(sub_ready, 1)

            def softmax_mul(b, i):
                t = 4 * b + i
                sv = S[:, i * NH * SK:(i + 1) * NH * SK].rearrange("p (h k) -> p h k", h=NH)
                pool.wait_ge(rd_ready, t + 1)
                nc.gpsimd.tensor_tensor(sv, sv, rd[:, i, :].unsqueeze(2).to_broadcast([P, NH, SK]),
                                        ALU.mult).then_inc(p_ready, 1)

            def iteration(b, prev, last):
                for i in range(PER):
                    softmax_sub(b, i)
                for i in range(PER):
                    softmax_mul(b, i)
                if not last:
                    power(b + 1, 0, ln1_var, ln1_power)
                if prev is not None:
                    scatter_pairs(prev)
                power(b, 1, ln2_var, ln2_power)

            iteration(0, None, False)
            with pool.Fori(1, B - 1) as b:
                iteration(b, b - 1, False)
            iteration(B - 1, B - 2, True)
            scatter_pairs(B - 1)

            def gather(j, s, it):
                pool.wait_ge(ld_list[s], 16 * (it + 1))
                pass_waits(pool)
                nc.gpsimd.indirect_dma_start(
                    out=G[:, s, :], out_offset=None, in_=xrows[:, :],
                    in_offset=bass.IndirectOffsetOnAxis(ap=fresh[:, s, 0:1], axis=0)).then_inc(ld_rows[s], 16)

            def keep_entry(s):
                nc.gpsimd.tensor_copy(entry[:, s, :], fresh[:, s, :]).then_inc(entry_ready, 1)

            pool.wait_ge(st_rows, 16 * NT)
            pool.wait_ge(st_base, 16 * NT)
            for s in range(RING):
                gather(s, s, 0)
            keep_entry(0)
            keep_entry(1)

            def step(it, s, ahead, keep=True):
                j = RING * it + s
                if ahead:
                    pool.wait_ge(eT_mm, j + 1)
                    gather(j + RING, s, it + 1)
                before = (s + 2) % RING
                if not (isinstance(j, int) and j == 0):
                    pool.wait_ge(added[before], 16 * (it + (1 if s else 0)))
                    pass_waits(pool)
                if keep:
                    keep_entry(before)
                pool.wait_ge(entry_ready, j + 1)
                pool.wait_ge(ey_ready, j + 1)
                pass_waits(pool)
                nc.gpsimd.indirect_dma_start(
                    out=out, out_offset=bass.IndirectOffsetOnAxis(ap=entry[:, s, 0:1], axis=0),
                    in_=Y[:, s, :], in_offset=None, compute_op=ALU.add,
                    bounds_check=ROWS - 1, oob_is_err=True).then_inc(added[s], 16)

            for s in range(RING):
                step(0, s, True)
            with pool.Fori(1, ROUNDS - 1) as it:
                for s in range(RING):
                    step(it, s, True)
            for s in range(RING):
                step(ROUNDS - 1, s, False, keep=s == 0)
            for s in range(RING):
                pool.wait_ge(added[s], 16 * ROUNDS)

        @block.scalar
        def _(act):
            def hi(dst, src, scale=1.0):
                return nc.scalar.activation(dst, src, ACT.Copy, scale=scale)

            def fill_k(b):
                for n in range(GH):
                    rows = slice(n * HD, (n + 1) * HD)
                    last = hi(kbdv[rows, :, :, n * SK:(n + 1) * SK],
                              kc[rows, :, :, bass.ds(b, 1), :].rearrange("p h g b k -> p h g (b k)"))
                    last.then_inc(k_filled, 1)

            def fill_v(b):
                for d in range(2):
                    for n in range(2):
                        rows = slice(d * SK, (d + 1) * SK)
                        at = n * SK + d * HD
                        src = vc[rows, :, bass.ds(b, 1), :].rearrange("p h b (g n) -> p h (b g) n", g=NG)
                        dst = vbdv[rows, :, n::2, at:at + HD]
                        hi(dst, src[:, :, :, at:at + HD]).then_inc(v_filled, 1)

            act.wait_ge(ld_kv, 32)
            hi(ctx_s[:, 0].rearrange("p b e k -> p (b e k)"), ctx_raw, S_CTX).then_inc(kv_hi, 1)
            hi(wkv_s[:, 0, :], wkv_raw, S_W).then_inc(kv_hi, 1)
            act.wait_ge(ld_gates, 16)
            nc.scalar.activation(gl[:, 2:4], gl[:, 0:2], ACT.Tanh).then_inc(tanh_gates, 1)

            def normalise(b, i, dst, step_ready, which):
                t = 4 * b + i
                nc.scalar.activation(dst[:, i * D:(i + 1) * D], x_tile(t), ACT.Identity,
                                     bias=ln[:, which, i, 3:4], scale=ln[:, which, i, 2:3]).then_inc(step_ready, 1)

            def norm1(b):
                act.wait_ge(ln1_stats, b + 1)
                for i in range(PER):
                    normalise(b, i, xn1, xn1_ready, 0)

            norm1(0)
            for g in range(NG):
                act.wait_ge(k_mm, g + 1)
                hi(kc[:, 0, g].rearrange("p b k -> p (b k)"), mm_bank[g][:, 0:B * SK], S_KV / (S_CTX * S_W)).then_inc(k_hi, 1)
            for b in range(B):
                act.wait_ge(v_mm, b + 1)
                hi(vc[:, 0, b, :], mm_bank[b][:, :], S_KV / (S_CTX * S_W)).then_inc(v_hi, 1)
            act.wait_ge(consts, CONSTS)
            act.wait_ge(k_lo, NG)
            fill_k(0)
            act.wait_ge(v_lo, B)
            fill_v(0)
            act.wait_ge(ld_wq, 16)
            hi(wq_s[:, 0:DC * D], wq_raw, S_W).then_inc(wq_hi, 1)
            act.wait_ge(ld_wout, 16)
            hi(wout_s[:, 0:DC * D], wout_raw, S_W).then_inc(wout_hi, 1)
            act.wait_ge(ld_gate, 16)
            hi(gate_s[:, 0].rearrange("p c e -> p (c e)"), gate_raw[:, :], S_W).then_inc(gate_hi, 1)

            def turned_hi(b, view, mm, done):
                for i in range(PER):
                    turned_hi_one(b, i, view, mm, done)

            def turned_hi_one(b, i, view, mm, done):
                act.wait_ge(mm, 4 * b + i + 1)
                hi(view[:, 0, :, i * P:(i + 1) * P],
                   turn_bank[i % 2][:, :].rearrange("p (c t) -> p c t", c=DC)).then_inc(done, 1)

            def scores_out(b, i):
                for h in range(2):
                    act.wait_ge(s_mm, 2 * (4 * b + i) + h + 1)
                    at = i * NH * SK + h * 512
                    nc.scalar.activation(S[:, at:at + 512], score_bank[h][:, :], ACT.Copy).then_inc(s_copied, 1)

            def exps(b, i):
                act.wait_ge(sub_ready, 4 * b + i + 1)
                si = S[:, i * NH * SK:(i + 1) * NH * SK]
                nc.scalar.activation(si, si, ACT.Exp, scale=float(HD) ** -0.5 / (S_Q * S_KV)).then_inc(exp_ready, 1)

            def tanh_h(b, i):
                act.wait_ge(h_mm, 4 * b + i + 1)
                nc.scalar.activation(th[:, i % 2, :], mm_bank[i % 2][:, 0:INTER], ACT.Tanh,
                                     scale=0.5 / (S_LN * S_W)).then_inc(th_ready, 1)

            def g_hi(b, i):
                act.wait_ge(gT_mm, 4 * b + i + 1)
                hi(gT[:, 0], turn_bank[i % 2][:, 0:IC * P].rearrange("p (c t) -> p c t", c=IC)).then_inc(gT_hi, 1)

            def router_exp(b):
                act.wait_ge(lg_out, b + 1)
                nc.scalar.activation(ex[:, :, :], lg[:, :, :], ACT.Exp, scale=1.0 / (S_LN * S_W)).then_inc(lg_exp, 1)

            def split_pieces(lo_, hi_):
                for k in range(lo_, hi_):
                    raw, whi, _ = w_piece(k)
                    act.wait_ge(ld_w[k % 4], 16 * (k // 4 + 1))
                    hi(whi, raw, S_W).then_inc(w_hi, 1)

            def feed_forward(b, softmax):
                turned_hi_one(b, 0, x2T, x2T_mm, x2T_hi)
                turned_hi_one(b, 1, x2T, x2T_mm, x2T_hi)
                softmax(0)
                turned_hi_one(b, 2, x2T, x2T_mm, x2T_hi)
                turned_hi_one(b, 3, x2T, x2T_mm, x2T_hi)
                softmax(1)
                router_exp(b)
                tanh_h(b, 0)
                tanh_h(b, 1)
                softmax(2)
                g_hi(b, 0)
                softmax(3)
                tanh_h(b, 2)
                g_hi(b, 1)
                tanh_h(b, 3)
                g_hi(b, 2)
                g_hi(b, 3)

            def iteration(b, prev, last):
                turned_hi(b, xTv, xT_mm, xT_hi)
                for g in range(NG):
                    act.wait_ge(q_mm, 4 * b + g + 1)
                    hi(qTv[:, 0, g, :], mm_bank[g][:, :], S_Q / (S_LN * S_W)).then_inc(q_hi, 1)
                if prev is None:
                    act.wait_ge(wout_lo, 1)
                for i in range(PER):
                    scores_out(b, i)
                if prev is None:
                    for i in range(PER):
                        exps(b, i)
                    act.wait_ge(ld_shared, 32)
                    for h in range(2):
                        at = E * WE + h * (HALF // 2)
                        hi(arena16[:, at:at + HALF // 2], shared_raw[h], S_W).then_inc(shared_hi, 1)
                else:
                    feed_forward(prev, lambda i: exps(b, i))
                if not last:
                    norm1(b + 1)
                    fill_k(b + 1)
                for i in range(PER):
                    for h in range(2):
                        act.wait_ge(pT_mm, 2 * (4 * b + i) + h + 1)
                        hi(PTv[:, 0, 4 * h:4 * h + 4, i * P:(i + 1) * P],
                           turn_bank[h][:, :].rearrange("p (r t) -> p r t", r=4)).then_inc(pT_hi, 1)
                for g in range(NG):
                    act.wait_ge(a_mm, 4 * b + g + 1)
                    hi(aTv[:, 0, g, :], mm_bank[g][:, :], S_A / (S_P * S_KV)).then_inc(a_hi, 1)
                if not last:
                    fill_v(b + 1)
                if prev is not None:
                    act.wait_ge(st_rows, 64 * b)
                act.wait_ge(ln2_stats, b + 1)
                for i in range(PER):
                    normalise(b, i, xn2, xn2_ready, 1)

            iteration(0, None, False)
            with act.Fori(1, B - 1) as b:
                iteration(b, b - 1, False)
            iteration(B - 1, B - 2, True)
            act.wait_ge(y_mm, NT)
            feed_forward(B - 1, lambda i: split_pieces(2 * i, 2 * i + 2))
            split_pieces(8, PIECES)

            def rows_hi(j, s):
                act.wait_ge(eT_mm, j + 1)
                hi(GT[:, s, 0], e_turn[:, :].rearrange("p (c t) -> p c t", c=DC)).then_inc(eT_hi, 1)

            def tanh_e(j, s):
                act.wait_ge(eh_mm, j + 1)
                nc.scalar.activation(th[:, s, :], e_h[s][:, 0:INTER], ACT.Tanh,
                                     scale=0.5 / (S_LN * S_W)).then_inc(eth_ready, 1)

            def step(it, s, turn=True, nxt=True):
                j = RING * it + s
                if turn:
                    rows_hi(j + 2, (s + 2) % RING)
                act.wait_ge(egT_mm, j + 1)
                hi(gT[:, 0], e_g[:, 0:IC * P].rearrange("p (c t) -> p c t", c=IC)).then_inc(egT_hi, 1)
                if nxt:
                    tanh_e(j + 1, (s + 1) % RING)
                act.wait_ge(ey_mm, j + 1)
                act.wait_ge(entry_ready, j + 1)
                if not isinstance(it, int) or it > 0:
                    act.wait_ge(added[s], 16 * it)
                nc.scalar.activation(Y[:, s, :], e_y[s][:, :], ACT.Copy,
                                     scale=entry[:, s, 1:2].bitcast(F32)).then_inc(ey_ready, 1)

            rows_hi(0, 0)
            rows_hi(1, 1)
            tanh_e(0, 0)
            for s in range(RING):
                step(0, s)
            with act.Fori(1, ROUNDS - 1) as it:
                for s in range(RING):
                    step(it, s)
            for s in range(RING):
                step(ROUNDS - 1, s, turn=s == 0, nxt=s < 2)

        @block.vector
        def _(dve):
            V = nc.vector

            def lo(dst, src, high, scale=1.0):
                if scale == 1.0:
                    return V.tensor_tensor(dst, src, high, ALU.subtract)
                return V.scalar_tensor_tensor(out=dst, in0=src, scalar=scale, in1=high, op0=ALU.mult, op1=ALU.subtract)

            dve.wait_ge(consts, CONSTS)
            V.tensor_scalar(empty[:, :, 0], empty[:, :, 0], P - 1, TOK, ALU.bitwise_and, ALU.bitwise_or).then_inc(zeroed, 1)
            dve.wait_ge(kv_hi, 2)
            lo(ctx_s[:, 1].rearrange("p b e k -> p (b e k)"), ctx_raw,
               ctx_s[:, 0].rearrange("p b e k -> p (b e k)"), S_CTX).then_inc(kv_lo, 1)
            lo(wkv_s[:, 1, :], wkv_raw, wkv_s[:, 0, :], S_W).then_inc(kv_lo, 1)

            STEPS = PER + 1

            def statistics(b, i, which, step_sem):
                t = 4 * b + i
                V.bn_stats(mv[:, which, i, 0:6], x_tile(t)).then_inc(step_sem, 1)
                dve.wait_ge(step_sem, STEPS * b + i + 1)

            def scale_and_bias(b, which, step_sem, var, power, done):
                w = ln[:, which]
                dve.wait_ge(step_sem, STEPS * b + PER)
                pass_waits(dve)
                for i in range(PER):
                    ins = V.bn_aggr(w[:, i, 0:2], mv[:, which, i, 0:6])
                ins.then_inc(step_sem, 1)
                dve.wait_ge(step_sem, STEPS * b + PER + 1)
                V.tensor_scalar(w[:, :, 1], w[:, :, 1], EPS, S_LN ** -2, ALU.add, ALU.mult).then_inc(var, 1)
                dve.wait_ge(power, b + 1)
                V.scalar_tensor_tensor(out=w[:, :, 3], in0=w[:, :, 0], scalar=-1.0, in1=w[:, :, 2],
                                       op0=ALU.mult, op1=ALU.mult).then_inc(done, 1)

            dve.wait_ge(ld_x0, 16)
            for i in range(PER):
                statistics(0, i, 0, ln1_step)
            scale_and_bias(0, 0, ln1_step, ln1_var, ln1_power, ln1_stats)
            dve.wait_ge(tanh_gates, 1)
            V.tensor_scalar(gl[:, 0:1], gl[:, 2:3], 1.0 / (S_A * S_W), None, ALU.mult).then_inc(gates_ready, 1)
            V.tensor_scalar(gl[:, 1:2], gl[:, 3:4], 1.0 / (S_G * S_W), None, ALU.mult).then_inc(gates_ready, 1)
            dve.wait_ge(gates_ready, 2)
            for g in range(NG):
                dve.wait_ge(k_hi, g + 1)
                lo(kc[:, 1, g].rearrange("p b k -> p (b k)"), mm_bank[g][:, 0:B * SK],
                   kc[:, 0, g].rearrange("p b k -> p (b k)"), S_KV / (S_CTX * S_W)).then_inc(k_lo, 1)
            for b in range(B):
                dve.wait_ge(v_hi, b + 1)
                lo(vc[:, 1, b, :], mm_bank[b][:, :], vc[:, 0, b, :], S_KV / (S_CTX * S_W)).then_inc(v_lo, 1)
            dve.wait_ge(wq_hi, 1)
            lo(wq_s[:, DC * D:2 * DC * D], wq_raw, wq_s[:, 0:DC * D], S_W).then_inc(wq_lo, 1)
            dve.wait_ge(wout_hi, 1)
            lo(wout_s[:, DC * D:2 * DC * D], wout_raw, wout_s[:, 0:DC * D], S_W).then_inc(wout_lo, 1)
            dve.wait_ge(gate_hi, 1)
            lo(gate_s[:, 1].rearrange("p c e -> p (c e)"), gate_raw[:, :],
               gate_s[:, 0].rearrange("p c e -> p (c e)"), S_W).then_inc(gate_lo, 1)
            dve.wait_ge(ld_x, 16)

            def turned_lo_one(b, i, view, high, done):
                dve.wait_ge(high, 4 * b + i + 1)
                lo(view[:, 1, :, i * P:(i + 1) * P], turn_bank[i % 2][:, :].rearrange("p (c t) -> p c t", c=DC),
                   view[:, 0, :, i * P:(i + 1) * P]).then_inc(done, 1)

            def head_max(b, i):
                if i == 0:
                    dve.wait_ge(masked, b + 1)
                else:
                    dve.wait_ge(s_copied, 2 * (4 * b + i) + 2)
                V.tensor_reduce(mx[:, i, :], S[:, i * NH * SK:(i + 1) * NH * SK].rearrange("p (h k) -> p h k", h=NH),
                                AX.X, ALU.max).then_inc(max_ready, 1)

            def head_sum(b, i):
                t = 4 * b + i
                dve.wait_ge(exp_ready, t + 1)
                V.tensor_reduce(mx[:, i, :], S[:, i * NH * SK:(i + 1) * NH * SK].rearrange("p (h k) -> p h k", h=NH),
                                AX.X, ALU.add).then_inc(sum_ready, 1)
                dve.wait_ge(sum_ready, 2 * t + 1)
                V.tensor_scalar(mx[:, i, :], mx[:, i, :], 1.0 / S_P, None, ALU.mult).then_inc(sum_ready, 1)
                dve.wait_ge(sum_ready, 2 * t + 2)
                V.reciprocal(rd[:, i, :], mx[:, i, :]).then_inc(rd_ready, 1)

            def over(v):
                return v.unsqueeze(2).to_broadcast([P, PER, E])

            def each_tile(v):
                return v.unsqueeze(1).to_broadcast([P, PER, E])

            lg_bank = mm_bank[3][:, 0:PER * E].rearrange("p (i e) -> p i e", i=PER)

            def router_logits(b):
                dve.wait_ge(lg_mm, b + 1)
                V.tensor_reduce(m[:, 0, :], lg_bank, AX.X, ALU.max).then_inc(lg_max, 1)
                dve.wait_ge(lg_max, b + 1)
                V.tensor_tensor(lg[:, :, :], lg_bank, over(m[:, 0, :]), ALU.subtract).then_inc(lg_out, 1)

            ROUTE = 13

            def router_choose(b):
                n = [0]

                def link(ins):
                    n[0] += 1
                    ins.then_inc(route_step, 1)
                    dve.wait_ge(route_step, ROUTE * b + n[0])

                dve.wait_ge(lg_exp, b + 1)
                link(V.tensor_reduce(m[:, 1, :], ex[:, :, :], AX.X, ALU.add))
                link(V.reciprocal(m[:, 2, :], m[:, 1, :]))
                link(V.tensor_tensor(sc[:, :, :], ex[:, :, :], over(m[:, 2, :]), ALU.mult))
                src = sc
                for k in range(2):
                    link(V.tensor_reduce(m[:, 3 + k, :], src[:, :, :], AX.X, ALU.max))
                    link(V.tensor_tensor(eq[:, :, :], src[:, :, :], over(m[:, 3 + k, :]), ALU.is_equal))
                    link(V.tensor_tensor(eq[:, :, :], eq[:, :, :], each_tile(first_high[:, :]), ALU.mult))
                    link(V.tensor_reduce(m[:, 5, :], eq[:, :, :], AX.X, ALU.max))
                    if k == 0:
                        link(V.tensor_tensor(oh[:, 0], eq[:, :, :], over(m[:, 5, :]), ALU.is_equal))
                        link(V.scalar_tensor_tensor(out=sc2[:, :, :], in0=oh[:, 0], scalar=-2.0, in1=sc[:, :, :],
                                                    op0=ALU.mult, op1=ALU.add))
                        src = sc2
                assert n[0] == ROUTE
                ins = V.tensor_tensor(oh[:, 1], eq[:, :, :], over(m[:, 5, :]), ALU.is_equal)
                ins.then_inc(route2_step, 1)
                dve.wait_ge(route2_step, ROUTE2 * b + 1)
                V.tensor_tensor(mask16[:, :].rearrange("p (i e) -> p i e", i=PER), oh[:, 0], oh[:, 1],
                                ALU.add).then_inc(mask_ready, 1)

            ROUTE2 = 9

            def router_place(b):
                n = [1]

                def link(ins):
                    n[0] += 1
                    ins.then_inc(route2_step, 1)
                    dve.wait_ge(route2_step, ROUTE2 * b + n[0])

                dve.wait_ge(pos_mm, b + 1)
                link(V.tensor_tensor(pos[:, :, :], mm_bank[0][:, 0:PER * E].rearrange("p (i e) -> p i e", i=PER),
                                     each_tile(seen[:, :]), ALU.add))
                V.tensor_tensor(seen[:, :], mm_bank[0][:, PER * E:PER * E + E], seen[:, :], ALU.add).then_inc(pos_out, 1)
                if not isinstance(b, int) or b > 0:
                    dve.wait_ge(st_pairs, 16 * 2 * PER * b)
                for k in range(2):
                    link(V.tensor_tensor(sel[:, :, :], pos[:, :, :], oh[:, k], ALU.mult))
                    link(V.tensor_reduce(slot[:, :, k], sel[:, :, :], AX.X, ALU.add))
                    link(V.tensor_scalar(pair[:, :, k, 1].bitcast(F32), m[:, 3 + k, :], gl[:, 1:2], None, ALU.mult))
                link(V.tensor_scalar(pair[:, :, :, 0], pair[:, :, :, 0], float(SQ), None, ALU.add))
                assert n[0] == ROUTE2
                V.tensor_copy(count[:, 0, :], seen[:, :]).then_inc(pairs_ready, 1)

            def hidden(b, i):
                t = 4 * b + i
                s = i % 2
                dve.wait_ge(th_ready, t + 1)
                V.scalar_tensor_tensor(out=uu[:, s, :], in0=th[:, s, :], scalar=1.0, in1=mm_bank[s][:, 0:INTER],
                                       op0=ALU.add, op1=ALU.mult).then_inc(u_ready, 1)
                dve.wait_ge(u_ready, t + 1)
                V.scalar_tensor_tensor(out=gg[:, s, :], in0=uu[:, s, :], scalar=0.5 * S_G / (S_LN * S_W) ** 2,
                                       in1=mm_bank[s][:, INTER:2 * INTER], op0=ALU.mult,
                                       op1=ALU.mult).then_inc(g_ready, 1)

            def g_lo(b, i):
                dve.wait_ge(gT_hi, 4 * b + i + 1)
                lo(gT[:, 1], turn_bank[i % 2][:, 0:IC * P].rearrange("p (c t) -> p c t", c=IC),
                   gT[:, 0]).then_inc(gT_lo, 1)

            def base(b, i):
                t = 4 * b + i
                dve.wait_ge(z_mm, t + 1)
                V.scalar_tensor_tensor(out=x_tile(t), in0=mm_bank[2 + i % 2][:, :], scalar=gl[:, 1:2],
                                       in1=x_tile(t), op0=ALU.mult, op1=ALU.add).then_inc(base_ready, 1)

            def split_pieces(lo_, hi_):
                for k in range(lo_, hi_):
                    raw, whi, wlo = w_piece(k)
                    dve.wait_ge(w_hi, k + 1)
                    lo(wlo, raw, whi, S_W).then_inc(w_lo, 1)

            def feed_forward(b, softmax_max, softmax_sum):
                softmax_max(0)
                turned_lo_one(b, 0, x2T, x2T_hi, x2T_lo)
                turned_lo_one(b, 1, x2T, x2T_hi, x2T_lo)
                softmax_max(1)
                turned_lo_one(b, 2, x2T, x2T_hi, x2T_lo)
                turned_lo_one(b, 3, x2T, x2T_hi, x2T_lo)
                softmax_max(2)
                softmax_max(3)
                router_logits(b)
                softmax_sum(0)
                hidden(b, 0)
                hidden(b, 1)
                router_choose(b)
                g_lo(b, 0)
                softmax_sum(1)
                hidden(b, 2)
                base(b, 0)
                g_lo(b, 1)
                softmax_sum(2)
                hidden(b, 3)
                base(b, 1)
                g_lo(b, 2)
                softmax_sum(3)
                base(b, 2)
                router_place(b)
                g_lo(b, 3)
                base(b, 3)

            def iteration(b, prev, last):
                for i in range(PER):
                    turned_lo_one(b, i, xTv, xT_hi, xT_lo)
                for g in range(NG):
                    dve.wait_ge(q_hi, 4 * b + g + 1)
                    lo(qTv[:, 1, g, :], mm_bank[g][:, :], qTv[:, 0, g, :], S_Q / (S_LN * S_W)).then_inc(q_lo, 1)
                if prev is None:
                    for i in range(PER):
                        head_max(b, i)
                    for i in range(PER):
                        head_sum(b, i)
                    for h in range(2):
                        at = E * WE + h * (HALF // 2)
                        dve.wait_ge(shared_hi, h + 1)
                        lo(arena16[:, at + HALF:at + HALF + HALF // 2], shared_raw[h],
                           arena16[:, at:at + HALF // 2], S_W).then_inc(shared_lo, 1)
                else:
                    feed_forward(prev, lambda i: head_max(b, i), lambda i: head_sum(b, i))
                if not last:
                    for i in range(PER):
                        statistics(b + 1, i, 0, ln1_step)
                    scale_and_bias(b + 1, 0, ln1_step, ln1_var, ln1_power, ln1_stats)
                for i in range(PER):
                    for h in range(2):
                        dve.wait_ge(pT_hi, 2 * (4 * b + i) + h + 1)
                        lo(PTv[:, 1, 4 * h:4 * h + 4, i * P:(i + 1) * P],
                           turn_bank[h][:, :].rearrange("p (r t) -> p r t", r=4),
                           PTv[:, 0, 4 * h:4 * h + 4, i * P:(i + 1) * P]).then_inc(pT_lo, 1)
                for g in range(NG):
                    dve.wait_ge(a_hi, 4 * b + g + 1)
                    lo(aTv[:, 1, g, :], mm_bank[g][:, :], aTv[:, 0, g, :], S_A / (S_P * S_KV)).then_inc(a_lo, 1)
                for i in range(PER):
                    t = 4 * b + i
                    dve.wait_ge(y_mm, t + 1)
                    V.scalar_tensor_tensor(out=x_tile(t), in0=mm_bank[i][:, :], scalar=gl[:, 0:1], in1=x_tile(t),
                                           op0=ALU.mult, op1=ALU.add).then_inc(x1_ready, 1)
                    dve.wait_ge(x1_ready, t + 1)
                    pass_waits(dve)
                    statistics(b, i, 1, ln2_step)
                scale_and_bias(b, 1, ln2_step, ln2_var, ln2_power, ln2_stats)

            iteration(0, None, False)
            with dve.Fori(1, B - 1) as b:
                iteration(b, b - 1, False)
            iteration(B - 1, B - 2, True)
            feed_forward(B - 1, lambda i: None, lambda i: split_pieces(2 * i, 2 * i + 2))

            n = [0]

            def link(ins):
                n[0] += 1
                ins.then_inc(table_step, 1)
                dve.wait_ge(table_step, n[0])

            r = slice(0, 1)

            def by_tile(v):
                return v.unsqueeze(1).to_broadcast([1, TILES, E])

            dve.wait_ge(pairs_ready, B)
            link(V.tensor_tensor(count[r, 1, :], count[r, 0, :], list_at[r, :], ALU.subtract))
            link(V.tensor_scalar(count_i[r, 0, :], count[r, 1, :], float(P - 1), None, ALU.add))
            link(V.tensor_scalar(count_i[r, 1, :], count_i[r, 0, :], 7, None, ALU.arith_shift_right))
            link(V.tensor_copy(count[r, 2, :], count_i[r, 1, :]))
            link(V.memset(count[r, 3, :], 1.0))
            link(V.tensor_tensor_scan(count[r, 4, :], count[r, 3, :], count[r, 2, :], 0.0, ALU.mult, ALU.add))
            link(V.tensor_scalar(count[r, 5, :], count[r, 2, :], -float(P), float(LIST), ALU.mult, ALU.add))
            link(V.tensor_tensor(past[r], tile_no[r, :].unsqueeze(2).to_broadcast([1, TILES, E]),
                                 by_tile(count[r, 4, :]), ALU.is_ge))
            link(V.tensor_reduce(tab[r, 0, :], past[r], AX.X, ALU.add))
            link(V.tensor_tensor(skip[r], past[r], by_tile(count[r, 5, :]), ALU.mult))
            link(V.tensor_reduce(tab_f[r, 0, :], skip[r], AX.X, ALU.add))
            link(V.scalar_tensor_tensor(out=tab_f[r, 1, :], in0=tile_no[r, :], scalar=float(P), in1=tab_f[r, 0, :],
                                        op0=ALU.mult, op1=ALU.add))
            V.tensor_copy(tab[r, 1, :], tab_f[r, 1, :]).then_inc(table_ready, 1)
            split_pieces(8, PIECES)

            def rows_lo(j, s):
                dve.wait_ge(eT_hi, j + 1)
                lo(GT[:, s, 1], e_turn[:, :].rearrange("p (c t) -> p c t", c=DC), GT[:, s, 0]).then_inc(eT_lo, 1)

            def hidden_e(j, s):
                dve.wait_ge(eth_ready, j + 1)
                V.scalar_tensor_tensor(out=uu[:, s, :], in0=th[:, s, :], scalar=1.0, in1=e_h[s][:, 0:INTER],
                                       op0=ALU.add, op1=ALU.mult).then_inc(eu_ready, 1)
                dve.wait_ge(eu_ready, j + 1)
                V.scalar_tensor_tensor(out=gg[:, s, :], in0=uu[:, s, :], scalar=0.5 * S_G / (S_LN * S_W) ** 2,
                                       in1=e_h[s][:, INTER:2 * INTER], op0=ALU.mult,
                                       op1=ALU.mult).then_inc(eg_ready, 1)

            def step(it, s, turn=True, nxt=True):
                j = RING * it + s
                if turn:
                    rows_lo(j + 2, (s + 2) % RING)
                dve.wait_ge(egT_hi, j + 1)
                lo(gT[:, 1], e_g[:, 0:IC * P].rearrange("p (c t) -> p c t", c=IC), gT[:, 0]).then_inc(egT_lo, 1)
                if nxt:
                    hidden_e(j + 1, (s + 1) % RING)

            rows_lo(0, 0)
            rows_lo(1, 1)
            hidden_e(0, 0)
            for s in range(RING):
                step(0, s)
            with dve.Fori(1, ROUNDS - 1) as it:
                for s in range(RING):
                    step(it, s)
            for s in range(RING):
                step(ROUNDS - 1, s, turn=s == 0, nxt=s < 2)

        @block.tensor
        def _(pe):
            def product(dst, pairs):
                steps = [(a(u), b(v)) for a, b in pairs for u, v in ((0, 0), (0, 1), (1, 0))]
                for n, (a, b) in enumerate(steps):
                    last = nc.tensor.matmul(dst, a, b, start=n == 0, stop=n == len(steps) - 1)
                return last

            def turn(dst, src, n):
                for c in range(n):
                    last = nc.tensor.transpose(dst[:, c * P:(c + 1) * P], src[:, c * P:(c + 1) * P], ident[:, :])
                return last

            pe.wait_ge(consts, 5)
            pe.wait_ge(kv_lo, 2)
            for g in range(NG):
                product(mm_bank[g][:, 0:B * SK].rearrange("p (b k) -> p b k", b=B),
                        [(lambda h, g=g: wkv_s[:, h, g * P:(g + 1) * P],
                          lambda h: ctx_s[:, h, :, 0, :])]).then_inc(k_mm, 1)
            for b in range(B):
                pe.wait_ge(k_lo, b + 1)
                product(mm_bank[b][:, :],
                        [(lambda h, b=b: ctx_s[:, h, b].rearrange("p e k -> p (e k)"),
                          lambda h: wkv_s[:, h, D:2 * D])]).then_inc(v_mm, 1)

            def router(b):
                for i in range(PER):
                    cols = mm_bank[3][:, i * E:(i + 1) * E]
                    last = product(cols, [(lambda h, c=c, i=i: x2T[:, h, c, i * P:(i + 1) * P],
                                           lambda h, c=c: gate_s[:, h, c, :]) for c in range(DC)])
                last.then_inc(lg_mm, 1)

            def shared_w(h, c):
                at = E * WE + h * HALF + c * D
                return arena16[:, at:at + D]

            def hidden(b, i):
                if i >= 2:
                    pe.wait_ge(g_ready, 4 * b + i - 1)
                product(mm_bank[i % 2][:, :], [(lambda h, c=c: x2T[:, h, c, i * P:(i + 1) * P],
                                                lambda h, c=c: shared_w(h, c)) for c in range(DC)]).then_inc(h_mm, 1)

            def turn_g(b, i):
                pe.wait_ge(g_ready, 4 * b + i + 1)
                if i >= 2:
                    pe.wait_ge(gT_lo, 4 * b + i - 1)
                turn(turn_bank[i % 2], gg[:, i % 2, :], IC).then_inc(gT_mm, 1)

            def down(b, i):
                pe.wait_ge(gT_lo, 4 * b + i + 1)
                if i == 1:
                    pe.wait_ge(lg_out, b + 1)
                if i >= 2:
                    pe.wait_ge(base_ready, 4 * b + i - 1)
                product(mm_bank[2 + i % 2][:, :], [(lambda h, c=c: gT[:, h, c, :],
                                                    lambda h, c=c: shared_w(h, DC + c))
                                                   for c in range(IC)]).then_inc(z_mm, 1)

            def count_pairs(b):
                pe.wait_ge(mask_ready, b + 1)
                pe.wait_ge(g_ready, 4 * b + 4)
                bank0 = mm_bank[0]
                nc.tensor.matmul(bank0[:, 0:PER * E], earlier[:, :], mask16[:, :], start=True, stop=False)
                for i in range(1, PER):
                    nc.tensor.matmul(bank0[:, i * E:PER * E], ones16[:, :], mask16[:, 0:(PER - i) * E],
                                     start=False, stop=i == PER - 1)
                for i in range(PER):
                    last = nc.tensor.matmul(bank0[:, PER * E:PER * E + E], ones16[:, :], mask16[:, i * E:(i + 1) * E],
                                            start=i == 0, stop=i == PER - 1)
                last.then_inc(pos_mm, 1)

            def feed_forward(b):
                for i in range(PER):
                    pe.wait_ge(xn2_ready, 4 * b + i + 1)
                    if i >= 2:
                        pe.wait_ge(x2T_lo, 4 * b + i - 1)
                    turn(turn_bank[i % 2], xn2[:, i * D:(i + 1) * D], DC).then_inc(x2T_mm, 1)
                pe.wait_ge(x2T_lo, 4 * b + 4)
                router(b)
                hidden(b, 0)
                hidden(b, 1)
                turn_g(b, 0)
                hidden(b, 2)
                down(b, 0)
                turn_g(b, 1)
                hidden(b, 3)
                down(b, 1)
                turn_g(b, 2)
                down(b, 2)
                turn_g(b, 3)
                count_pairs(b)
                down(b, 3)

            def iteration(b, prev):
                for i in range(PER):
                    pe.wait_ge(xn1_ready, 4 * b + i + 1)
                    if i >= 2:
                        pe.wait_ge(xT_lo, 4 * b + i - 1)
                    turn(turn_bank[i % 2], xn1[:, i * D:(i + 1) * D], DC).then_inc(xT_mm, 1)
                if prev is None:
                    pe.wait_ge(wq_lo, 1)
                pe.wait_ge(xT_lo, 4 * b + 4)
                for g in range(NG):
                    if prev is None:
                        pe.wait_ge(v_lo, g + 1)
                    else:
                        pe.wait_ge(x1_ready, 4 * b + g - 3)
                    product(mm_bank[g][:, :], [(lambda h, c=c: wqv[:, h, c, g * P:(g + 1) * P],
                                                lambda h, c=c: xTv[:, h, c, :]) for c in range(DC)]).then_inc(q_mm, 1)
                pe.wait_ge(q_lo, 4 * b + 4)
                pe.wait_ge(k_filled, GH * (b + 1))
                for i in range(PER):
                    for half in range(2):
                        if not (prev is None and i == 0):
                            pe.wait_ge(s_copied, 2 * (4 * b + i) + half - 1)
                        for g in (2 * half, 2 * half + 1):
                            last = product(score_bank[half][:, (g % 2) * 256:(g % 2 + 1) * 256],
                                           [(lambda h: qTv[:, h, g, i * P:(i + 1) * P], lambda h: kbdv[:, h, g, :])])
                        last.then_inc(s_mm, 1)
                if prev is not None:
                    feed_forward(prev)
                for i in range(PER):
                    t = 4 * b + i
                    pe.wait_ge(p_ready, t + 1)
                    for h in range(2):
                        if i >= 1:
                            pe.wait_ge(pT_lo, 2 * t + h - 1)
                        elif prev is not None:
                            pe.wait_ge(gT_lo, 4 * b)
                        turn(turn_bank[h], S[:, i * NH * SK + h * 512:i * NH * SK + h * 512 + 512], 4).then_inc(pT_mm, 1)
                pe.wait_ge(pT_lo, 2 * (4 * b + 4))
                pe.wait_ge(v_filled, 4 * (b + 1))
                if prev is not None:
                    pe.wait_ge(base_ready, 4 * b)
                    pe.wait_ge(pos_out, b)
                for g in range(NG):
                    product(mm_bank[g][:, :], [(lambda h, r=r: vbdv[:, h, r, :], lambda h, r=r: PTv[:, h, r, :])
                                               for r in (2 * g, 2 * g + 1)]).then_inc(a_mm, 1)
                pe.wait_ge(a_lo, 4 * b + 4)
                if prev is None:
                    pe.wait_ge(wout_lo, 1)
                for i in range(PER):
                    product(mm_bank[i][:, :], [(lambda h, g=g: aTv[:, h, g, i * P:(i + 1) * P],
                                                lambda h, g=g: woutv[:, h, g, :]) for g in range(NG)]).then_inc(y_mm, 1)

            iteration(0, None)
            pe.wait_ge(gate_lo, 1)
            pe.wait_ge(shared_lo, 2)
            with pe.Fori(1, B) as b:
                iteration(b, b - 1)
            feed_forward(B - 1)

            def expert_of(j):
                return nc.values_load(tab[0:1, 0, bass.ds(j, 1)], engines=[PE_ENGINE], min_val=0, max_val=E,
                                      skip_runtime_bounds_check_because="a count of experts passed, at most E")

            def w_at(e, h, c):
                return arena16[:, bass.ds(e * WE + (h * HALF + c * D), D)]

            def turn_rows(j, s, it):
                pe.wait_ge(ld_rows[s], 16 * (it + 1))
                if not isinstance(j, int) or j > 0:
                    pe.wait_ge(eT_lo, j)
                turn(e_turn, G[:, s, :], DC).then_inc(eT_mm, 1)

            def hidden_e(j, s):
                e = expert_of(j)
                pe.wait_ge(eT_lo, j + 1)
                product(e_h[s][:, :], [(lambda h, c=c: GT[:, s, h, c, :], lambda h, c=c: w_at(e, h, c))
                                       for c in range(DC)]).then_inc(eh_mm, 1)

            def step(it, s, turn_=True, nxt=True):
                j = RING * it + s
                if turn_:
                    turn_rows(j + 2, (s + 2) % RING, it + (s + 2) // RING)
                pe.wait_ge(eg_ready, j + 1)
                if not isinstance(j, int) or j > 0:
                    pe.wait_ge(egT_lo, j)
                turn(e_g, gg[:, s, :], IC).then_inc(egT_mm, 1)
                if nxt:
                    hidden_e(j + 1, (s + 1) % RING)
                e = expert_of(j)
                pe.wait_ge(egT_lo, j + 1)
                if not isinstance(it, int) or it > 0:
                    pe.wait_ge(ey_ready, j - 2)
                product(e_y[s][:, :], [(lambda h, c=c: gT[:, h, c, :], lambda h, c=c: w_at(e, h, DC + c))
                                       for c in range(IC)]).then_inc(ey_mm, 1)

            pe.wait_ge(base_ready, NT)
            pe.wait_ge(pos_out, B)
            pe.wait_ge(table_ready, 1)
            turn_rows(0, 0, 0)
            turn_rows(1, 1, 0)
            pe.wait_ge(w_lo, PIECES)
            hidden_e(0, 0)
            for s in range(RING):
                step(0, s)
            with pe.Fori(1, ROUNDS - 1) as it:
                for s in range(RING):
                    step(it, s)
            for s in range(RING):
                step(ROUNDS - 1, s, turn_=s == 0, nxt=s < 2)


def kernel(**inputs):
    import concourse.bacc as bacc
    from concourse.bass_utils import run_bass_kernel_spmd

    v = {n: np.asarray(a) for n, a in inputs.items()}

    def chunks(w):
        return w.reshape(-1, P, w.shape[1]).transpose(1, 0, 2).reshape(P, -1)

    def expert(w1, w2, w3):
        up = np.concatenate([w1.T, w3.T], axis=1)
        return np.concatenate([chunks(up), chunks(w2.T)], axis=1)

    ctx_t = v["ctx_512"].transpose(2, 0, 1)
    arrays = {
        "x": v["x"].reshape(NT, P, D).transpose(1, 0, 2),
        "ctx_rows": np.stack([ctx_t, ctx_t], axis=2),
        "gates": np.broadcast_to(np.concatenate([v["g_xattn"], v["g_ffn"]])[None, :], (P, 2)),
        "wq": chunks(v["L0_xattn_Wq"].T),
        "wkv": v["L0_xattn_Wkv_expand"].T,
        "wout": chunks(v["L0_xattn_Wout"].T),
        "gate_w": chunks(v["L0_ffn_gate_w"].T),
        "experts": np.stack([expert(v["L0_ffn_w1"][e], v["L0_ffn_w2"][e], v["L0_ffn_w3"][e]) for e in range(E)]
                            + [expert(v["L0_ffn_ws1"], v["L0_ffn_ws2"], v["L0_ffn_ws3"])]),
    }
    arrays = {n: np.ascontiguousarray(a) for n, a in arrays.items()}
    nc = bacc.Bacc("TRN2", target_bir_lowering=False, num_devices=1)
    args = [nc.dram_tensor("in_" + n, a.shape, mybir.dt.from_np(a.dtype), kind="ExternalInput").ap()
            for n, a in arrays.items()]
    out = nc.dram_tensor("out", (ROWS, D), F32, kind="ExternalOutput").ap()
    block_program(nc, *args, out)
    r = run_bass_kernel_spmd(nc, [{"in_" + n: a for n, a in arrays.items()}], core_ids=[0])
    return r.results[0]["out"][:TOK].reshape(B, SQ, D)
```

```python
from contextlib import ExitStack

import numpy as np
import concourse.bass as bass
import concourse.mybir as mybir

F32 = mybir.dt.float32
F16 = mybir.dt.float16
I32 = mybir.dt.int32
ALU = mybir.AluOpType
ACT = mybir.ActivationFunctionType
AX = mybir.AxisListType
PE_ENGINE = mybir.EngineType.PE
SP_ENGINE = mybir.EngineType.SP

P = 128
B, SQ, D = 4, 512, 512
SK, L = 64, 128
NH, HD = 16, 32
E, INTER = 8, 256
TOK = B * SQ
NT = TOK // P
PER = SQ // P
DC = D // P
IC = INTER // P
GH = P // HD
NG = NH // GH
PR = NH // 2
EPS = 1e-5

LIST = TOK
TILES = 2 * TOK // P + E - 1
LISTS = E * LIST + E * P
ROWS = TOK + P
RING = 3
ROUNDS = TILES // RING
assert ROUNDS * RING == TILES

S_LN = 16.0
S_W = 256.0
S_CTX = 16.0
S_Q = 16.0
S_KV = 128.0
S_P = 1024.0
S_A = 128.0
S_G = 16.0
FILL = -3.0e38
WE = 2 * (DC + IC) * D
HALF = WE // 2


def block_program(nc, x, ctx_rows, gates, wq, wkv, wout, gate_w, experts, out):
    with ExitStack() as stack:
        def sb(name, shape, dt=F32):
            return stack.enter_context(nc.sbuf_tensor(name, shape, dt))

        def sem(name):
            return stack.enter_context(nc.semaphore(name))

        xrows = nc.dram_tensor("xrows", (ROWS, D), F32)
        lists = nc.dram_tensor("lists", (LISTS, 2), I32)

        arena = sb("arena", [P, (E + 1) * WE // 2])
        arena16 = arena[:, :].bitcast(F16)
        taken = [0]

        def part(n, dt=F32):
            at = taken[0]
            taken[0] = at + n
            assert taken[0] <= E * WE // 2
            v = arena[:, at:at + n]
            return v if dt == F32 else v.bitcast(dt)

        xT = part(DC * SQ, F16)
        xn1 = part(PER * D)
        wq_s = part(DC * D, F16)
        qT = part(NG * SQ, F16)
        kc = part(NG * B * SK, F16).rearrange("p (h g b k) -> p h g b k", h=2, g=NG, b=B)
        kbd = part(NG * GH * SK, F16)
        S = part(PER * NH * SK)
        PT = part(PR * SQ, F16)
        aT = part(NG * SQ, F16)
        wout_s = part(DC * D, F16)
        vc = part(B * D, F16).rearrange("p (h b n) -> p h b n", h=2, b=B)
        vbd = sb("vbd", [P, 2 * PR * P], F16)
        PTv = PT.rearrange("p (h r t) -> p h r t", h=2, r=PR)
        xTv = xT.rearrange("p (h c t) -> p h c t", h=2, c=DC)
        qTv = qT.rearrange("p (h g t) -> p h g t", h=2, g=NG)
        aTv = aT.rearrange("p (h g t) -> p h g t", h=2, g=NG)
        wqv = wq_s.rearrange("p (h c n) -> p h c n", h=2, c=DC)
        woutv = wout_s.rearrange("p (h c n) -> p h c n", h=2, c=DC)
        kbdv = kbd.rearrange("p (h g m) -> p h g m", h=2, g=NG)
        vbdv = vbd[:, :].rearrange("p (h r m) -> p h r m", h=2, r=PR)
        wq_raw = S[:, 0:DC * D]
        wout_raw = S[:, DC * D:2 * DC * D]
        wkv_raw = PT[:, 0:4 * D].bitcast(F32)
        ctx_raw = PT[:, 4 * D:4 * D + 4 * B * SK].bitcast(F32)

        wkv_s = sb("wkv_s", [P, 2, 2 * D], F16)
        ctx_s = sb("ctx_s", [P, 2, B, 2, SK], F16)
        gate_raw = sb("gate_raw", [P, DC * E])
        gate_s = sb("gate_s", [P, 2, DC, E], F16)
        x_sb = sb("x_sb", [P, NT * D])
        xn2 = sb("xn2", [P, PER * D])
        x2T = sb("x2T", [P, 2, DC, SQ], F16)
        th = sb("th", [P, RING, INTER])
        uu = sb("uu", [P, RING, INTER])
        gg = sb("gg", [P, RING, INTER])
        gT = sb("gT", [P, 2, 2, IC, P], F16)
        G = sb("G", [P, RING, D])
        GT = sb("GT", [P, RING, 2, DC, P], F16)
        shared_raw = [G[:, :, :].rearrange("p s d -> p (s d)"),
                      GT[:, :, :, :, :].rearrange("p s h c t -> p (s h c t)").bitcast(F32)]
        Y = sb("Y", [P, RING, D])
        fresh = sb("fresh", [P, RING, 2], I32)
        entry = sb("entry", [P, RING, 2], I32)
        ident = sb("ident", [P, P])
        earlier = sb("earlier", [P, P], F16)
        ones16 = sb("ones16", [P, P], F16)
        mv = sb("mv", [P, NT, 8])
        ln1 = sb("ln1", [P, NT, 4])
        ln2 = sb("ln2", [P, PER, 4])
        minus_half = sb("minus_half", [P, NT])
        mx = sb("mx", [P, PER, NH])
        rd = sb("rd", [P, PER, NH])
        gl = sb("gl", [P, 4])
        lg = sb("lg", [P, PER, E])
        ex = sb("ex", [P, PER, E])
        sc = sb("sc", [P, PER, E])
        sc2 = sb("sc2", [P, PER, E])
        eq = sb("eq", [P, PER, E])
        oh = sb("oh", [P, 2, PER, E])
        pos = sb("pos", [P, PER, E])
        sel = sb("sel", [P, PER, E])
        m = sb("m", [P, 6, PER])
        mask16 = sb("mask16", [P, PER * E], F16)
        first_high = sb("first_high", [P, E])
        list_at = sb("list_at", [P, E])
        seen = sb("seen", [P, E])
        slot = sb("slot", [P, PER, 2], I32)
        pair = sb("pair", [P, PER, 2, 2], I32)
        empty = sb("empty", [P, LISTS // P, 2], I32)
        count = sb("count", [P, 6, E])
        count_i = sb("count_i", [P, 2, E], I32)
        tile_no = sb("tile_no", [P, TILES])
        past = sb("past", [P, TILES, E])
        skip = sb("skip", [P, TILES, E])
        tab_f = sb("tab_f", [P, 2, TILES])
        tab = sb("tab", [P, 2, TILES], I32)

        bank = [stack.enter_context(nc.psum_tensor(f"bank{n}", [P, 512], F32)) for n in range(8)]
        score_bank, turn_bank, mm_bank = bank[0:2], bank[2:4], bank[4:8]
        e_turn, e_h, e_g, e_y = bank[0], bank[1:4], bank[4], bank[5:8]

        ld_gates, ld_kv, ld_x0, ld_x1, ld_x, ld_wq, ld_wout, ld_gate = (sem(n) for n in (
            "ld_gates", "ld_kv", "ld_x0", "ld_x1", "ld_x", "ld_wq", "ld_wout", "ld_gate"))
        ld_shared = sem("ld_shared")
        ld_w = [sem(f"ld_w{n}") for n in range(4)]
        passed = sem("passed")
        consts = sem("consts")
        zeroed = sem("zeroed")
        tanh_gates, gates_ready = sem("tanh_gates"), sem("gates_ready")
        kv_hi, kv_lo = sem("kv_hi"), sem("kv_lo")
        wq_hi, wq_lo, wout_hi, wout_lo = sem("wq_hi"), sem("wq_lo"), sem("wout_hi"), sem("wout_lo")
        gate_hi, gate_lo, shared_hi, shared_lo = (sem(n) for n in ("gate_hi", "gate_lo", "shared_hi", "shared_lo"))
        k_mm, k_hi, k_lo, v_mm, v_hi, v_lo = (sem(n) for n in ("k_mm", "k_hi", "k_lo", "v_mm", "v_hi", "v_lo"))
        k_filled, v_filled = sem("k_filled"), sem("v_filled")
        ln1_step, ln1_stats, xn1_ready = sem("ln1_step"), sem("ln1_stats"), sem("xn1_ready")
        ln1_var, ln1_power, ln2_var, ln2_power = (sem(n) for n in ("ln1_var", "ln1_power", "ln2_var", "ln2_power"))
        turned, turned_hi, turned_lo = sem("turned"), sem("turned_hi"), sem("turned_lo")
        q_mm, q_hi, q_lo = sem("q_mm"), sem("q_hi"), sem("q_lo")
        s_mm, s_copied, masked, max_ready, sub_ready, exp_ready, sum_ready, rd_ready, p_ready = (sem(n) for n in (
            "s_mm", "s_copied", "masked", "max_ready", "sub_ready", "exp_ready", "sum_ready", "rd_ready", "p_ready"))
        a_mm, a_hi, a_lo = sem("a_mm"), sem("a_hi"), sem("a_lo")
        y_mm, x1_ready = sem("y_mm"), sem("x1_ready")
        ln2_step, ln2_stats, xn2_ready = sem("ln2_step"), sem("ln2_stats"), sem("xn2_ready")
        lg_mm, lg_max, lg_out, lg_exp = sem("lg_mm"), sem("lg_max"), sem("lg_out"), sem("lg_exp")
        route_step, mask_ready, pos_mm, route2_step, pos_out, pairs_ready = (sem(n) for n in (
            "route_step", "mask_ready", "pos_mm", "route2_step", "pos_out", "pairs_ready"))
        h_mm, th_ready, u_ready, g_ready = sem("h_mm"), sem("th_ready"), sem("u_ready"), sem("g_ready")
        z_mm, base_ready = sem("z_mm"), sem("base_ready")
        st_rows, st_base, st_pairs, st_init = sem("st_rows"), sem("st_base"), sem("st_pairs"), sem("st_init")
        w_hi = sem("w_hi")
        w_split = [sem(f"w_split{n}") for n in range(4)]
        table_step, table_ready = sem("table_step"), sem("table_ready")
        ld_list = [sem(f"ld_list{n}") for n in range(RING)]
        ld_rows = [sem(f"ld_rows{n}") for n in range(RING)]
        added = [sem(f"added{n}") for n in range(RING)]
        eT_mm, eT_hi, eT_lo = sem("eT_mm"), sem("eT_hi"), sem("eT_lo")
        eh_mm, eth_ready, eu_ready, eg_ready = sem("eh_mm"), sem("eth_ready"), sem("eu_ready"), sem("eg_ready")
        egT_mm, egT_hi, egT_lo = sem("egT_mm"), sem("egT_hi"), sem("egT_lo")
        ey_mm, ey_ready, entry_ready = sem("ey_mm"), sem("ey_ready"), sem("entry_ready")

        def x_tile(t):
            return x_sb[:, bass.ds(t * D, D)]

        def w_slot(k):
            return k if k < 2 else (k - 2) % 4

        def w_round(k):
            return sum(w_slot(n) == w_slot(k) for n in range(k + 1))

        def w_piece(k):
            e, h = divmod(k, 2)
            at = e * WE + h * (HALF // 2)
            raw = x_sb[:, w_slot(k) * (HALF // 2):(w_slot(k) + 1) * (HALF // 2)]
            return raw, arena16[:, at:at + HALF // 2], arena16[:, at + HALF:at + HALF + HALF // 2]

        def turn_no(b, kind, i):
            if b is None:
                return i + 1, turn_bank[i % 2]
            first = isinstance(b, int) and b == 0
            last = isinstance(b, int) and b >= B - 1
            if first:
                at = {"x": i, "p": PER + i}[kind]
                start = PER
            else:
                at = {"x2": i, "g": PER + i if last else PER + 2 * i, "x": PER + 1 + 2 * i,
                      "p": (2 if last else 3) * PER + i}[kind]
                start = 4 * PER + 5 * PER * (b - 1)
                if isinstance(b, int) and b == B:
                    start = start - PER
            return start + at + 1, turn_bank[at % 2]

        MIX_FIRST = (("q", 0), ("q", 1), ("q", 2), ("p", 0), ("q", 3), ("p", 1), ("p", 2), ("p", 3))
        MIX = tuple((kind, i) for i in range(PER) for kind in "pq")
        MIX_LAST = tuple(("p", i) for i in range(PER))

        def mix(b):
            if isinstance(b, int) and b == 0:
                return MIX_FIRST
            return MIX_LAST if isinstance(b, int) and b == B - 1 else MIX

        LN1_GROUPS = ((0, PER), (PER, 2 * PER), (2 * PER, NT))

        PIECES = 2 * E
        LO_BY_POOL = (0, 1, 4, 6, 8, 10, 12, 14)
        CONSTS = 15

        def turn_halves(make, kind, i, src):
            if kind == "p":
                r = 4 * (i % 2)
                at = slice((i // 2) * P, (i // 2 + 1) * P)
                dst = [PTv[:, h, r:r + 4, at] for h in range(2)]
            elif kind == "g":
                dst = [gT[:, i % 2, h] for h in range(2)]
            else:
                dst = [(x2T if kind == "x2" else xTv)[:, h, :, i * P:(i + 1) * P] for h in range(2)]
            n = dst[0].shape[1]
            src = src[:, 0:n * P].rearrange("p (c t) -> p c t", c=n)
            return make(dst, src)

        def pass_waits(eng):
            eng.sem_inc(passed, 1)

        stack.enter_context(nc.allow_low_precision(reason="sums of whole numbers below 2^24, written as int32"))
        block = stack.enter_context(nc.Block())

        @block.sync
        def _(sp):
            sp.dma_start(ctx_raw.rearrange("p (b e k) -> p b e k", b=B, e=2), ctx_rows).then_inc(ld_kv, 16)
            sp.dma_start(wkv_raw, wkv).then_inc(ld_kv, 16)
            sp.dma_start(x_sb[:, 0:PER * D].rearrange("p (t d) -> p t d", t=PER), x[:, 0:PER, :]).then_inc(ld_x0, 16)
            sp.dma_start(gl[:, 0:2], gates).then_inc(ld_gates, 16)
            sp.dma_start(wq_raw, wq).then_inc(ld_wq, 16)
            sp.dma_start(x_sb[:, PER * D:2 * PER * D].rearrange("p (t d) -> p t d", t=PER),
                         x[:, PER:2 * PER, :]).then_inc(ld_x1, 16)
            sp.dma_start(wout_raw, wout).then_inc(ld_wout, 16)
            sp.dma_start(gate_raw[:, :], gate_w).then_inc(ld_gate, 16)
            sp.dma_start(x_sb[:, 2 * PER * D:NT * D].rearrange("p (t d) -> p t d", t=NT - 2 * PER),
                         x[:, 2 * PER:NT, :]).then_inc(ld_x, 16)
            for h in range(2):
                sp.dma_start(shared_raw[h], experts[E][:, h * (HALF // 2):(h + 1) * (HALF // 2)]).then_inc(ld_shared, 16)
            sp.wait_ge(zeroed, 1)
            sp.dma_start(xrows[TOK:ROWS, :], Y[:, 0, :]).then_inc(st_init, 16)
            sp.dma_start(out[TOK:ROWS, :], Y[:, 0, :]).then_inc(st_init, 16)
            sp.wait_ge(zeroed, 2)
            sp.dma_start(lists[:, :].rearrange("(p f) c -> p (f c)", p=P),
                         empty[:, :, :].rearrange("p f c -> p (f c)")).then_inc(st_init, 16)

            def store_base(b):
                for i in range(PER):
                    sp.wait_ge(base_ready, 4 * b + i + 1)
                    sp.dma_start(out[bass.ds((4 * b + i) * P, P), :], x_tile(4 * b + i)).then_inc(st_base, 16)

            def store_rows(b):
                for i in range(PER):
                    sp.wait_ge(xn2_ready, 4 * b + i + 1)
                    sp.dma_start(xrows[bass.ds((4 * b + i) * P, P), :],
                                 xn2[:, i * D:(i + 1) * D]).then_inc(st_rows, 16)

            store_rows(0)
            with sp.Fori(1, B - 1) as b:
                store_base(b - 1)
                store_rows(b)

            def load_pieces(lo, hi):
                for k in range(lo, hi):
                    s = w_slot(k)
                    if w_round(k) > 1:
                        sp.wait_ge(w_split[s], w_round(k) - 1)
                    sp.dma_start(w_piece(k)[0], experts[k // 2][:, (k % 2) * (HALF // 2):(k % 2 + 1) * (HALF // 2)]
                                 ).then_inc(ld_w[s], 16)

            sp.wait_ge(st_base, 16 * PER * (B - 2))
            load_pieces(0, 2)
            store_base(B - 2)
            load_pieces(2, 4)
            sp.wait_ge(st_base, 16 * PER * (B - 1))
            load_pieces(4, 9)
            store_rows(B - 1)
            load_pieces(9, PIECES)
            store_base(B - 1)

            sp.wait_ge(table_ready, 1)
            sp.wait_ge(st_init, 48)
            sp.wait_ge(st_pairs, 16 * 2 * NT)

            def load_list(j, s):
                at = nc.values_load(tab[0:1, 1, bass.ds(j, 1)], engines=[SP_ENGINE], min_val=0, max_val=LISTS - P,
                                    skip_runtime_bounds_check_because="tiles end within the lists and their spare part")
                sp.dma_start(fresh[:, s, :], lists[bass.ds(at, P), :]).then_inc(ld_list[s], 16)

            for s in range(RING):
                load_list(s, s)

            def list_step(it, s):
                j = RING * it + s
                sp.wait_ge(entry_ready, j + 1)
                sp.wait_ge(ld_rows[s], 16 * (it + 1))
                load_list(j + RING, s)

            for s in range(RING):
                list_step(0, s)
            with sp.Fori(1, ROUNDS - 1) as it:
                for s in range(RING):
                    list_step(it, s)

        @block.gpsimd
        def _(pool):
            pool.memset(ident[:, :], 0.0).then_inc(consts, 1)
            pool.memset(earlier[:, :], 1.0).then_inc(consts, 1)
            pool.memset(ones16[:, :], 1.0).then_inc(consts, 1)
            pool.wait_ge(consts, 3)
            pool.affine_select(out=ident[:, :], in_=ident[:, :], compare_op=ALU.not_equal, fill=1.0,
                               base=0, pattern=[[-1, P]], channel_multiplier=1).then_inc(consts, 1)
            pool.affine_select(out=earlier[:, :], in_=earlier[:, :], compare_op=ALU.is_gt, fill=0.0,
                               base=0, pattern=[[1, P]], channel_multiplier=-1).then_inc(consts, 1)
            pool.memset(kbd.bitcast(F32), 0.0).then_inc(consts, 1)
            pool.memset(vbd[:, :].bitcast(F32), 0.0).then_inc(consts, 1)
            pool.iota(first_high[:, :], pattern=[[-1, E]], base=E, channel_multiplier=0,
                      allow_small_or_imprecise_dtypes=True).then_inc(consts, 1)
            pool.iota(list_at[:, :], pattern=[[LIST, E]], base=0, channel_multiplier=0,
                      allow_small_or_imprecise_dtypes=True).then_inc(consts, 1)
            pool.iota(seen[:, :], pattern=[[LIST, E]], base=0, channel_multiplier=0,
                      allow_small_or_imprecise_dtypes=True).then_inc(consts, 1)
            pool.iota(pair[:, :, :, 0], pattern=[[P, PER], [0, 2]], base=-SQ, channel_multiplier=1).then_inc(consts, 1)
            pool.iota(tile_no[:, :], pattern=[[1, TILES]], base=0, channel_multiplier=0,
                      allow_small_or_imprecise_dtypes=True).then_inc(consts, 1)
            pool.memset(minus_half[:, :], -0.5).then_inc(consts, 1)
            pool.memset(Y[:, 0, :], 0.0).then_inc(zeroed, 1)
            pool.iota(empty[:, :, 0], pattern=[[1, LISTS // P]], base=0,
                      channel_multiplier=LISTS // P).then_inc(consts, 1)
            pool.memset(empty[:, :, 1], 0).then_inc(consts, 1)

            def power(w, var, done, n):
                pool.wait_ge(var, n)
                nc.gpsimd.tensor_tensor(w[:, :, 2], w[:, :, 1], minus_half[:, 0:w.shape[1]], ALU.pow).then_inc(done, 1)

            def power1(k):
                power(ln1[:, LN1_GROUPS[k][0]:LN1_GROUPS[k][1], :], ln1_var, ln1_power, k + 1)

            def power2(b, p):
                power(ln2[:, 2 * p:2 * p + 2, :], ln2_var, ln2_power, 2 * b + p + 1)

            pool.wait_ge(consts, CONSTS)
            power1(0)

            def scatter_pairs(b):
                pool.wait_ge(st_init, 48)
                pool.wait_ge(pairs_ready, b + 1)
                pass_waits(pool)
                for i in range(PER):
                    for k in range(2):
                        nc.gpsimd.indirect_dma_start(
                            out=lists[:, :], out_offset=bass.IndirectOffsetOnAxis(ap=slot[:, i, k:k + 1], axis=0),
                            in_=pair[:, i, k, :], in_offset=None).then_inc(st_pairs, 16)

            def softmax_sub(b, i):
                t = 4 * b + i
                si = S[:, i * NH * SK:(i + 1) * NH * SK]
                sv = si.rearrange("p (h k) -> p h k", h=NH)
                if i == 0:
                    pool.wait_ge(s_copied, 2 * t + 2)
                    pass_waits(pool)
                    pool.affine_select(out=sv, in_=sv, compare_op=ALU.is_ge, fill=FILL, base=0,
                                       pattern=[[0, NH], [-1, SK]], channel_multiplier=1).then_inc(masked, 1)
                pool.wait_ge(max_ready, t + 1)
                nc.gpsimd.tensor_tensor(sv, sv, mx[:, i, :].unsqueeze(2).to_broadcast([P, NH, SK]),
                                        ALU.subtract).then_inc(sub_ready, 1)

            def softmax_mul(b, i):
                t = 4 * b + i
                sv = S[:, i * NH * SK:(i + 1) * NH * SK].rearrange("p (h k) -> p h k", h=NH)
                pool.wait_ge(rd_ready, t + 1)
                nc.gpsimd.tensor_tensor(sv, sv, rd[:, i, :].unsqueeze(2).to_broadcast([P, NH, SK]),
                                        ALU.mult).then_inc(p_ready, 1)

            def split_piece(k):
                raw, whi, wlo = w_piece(k)
                pool.wait_ge(w_hi, k + 1)
                nc.gpsimd.tensor_tensor(wlo, raw, whi, ALU.subtract).then_inc(w_split[w_slot(k)], 1)

            def iteration(b, prev, nxt):
                softmax_sub(b, 3)
                for i in range(PER):
                    softmax_mul(b, i)
                if prev is None:
                    power1(2)
                else:
                    if not nxt:
                        split_piece(0)
                        split_piece(1)
                    scatter_pairs(prev)
                if nxt:
                    softmax_sub(b + 1, 0)
                else:
                    split_piece(4)
                power2(b, 0)
                if nxt:
                    softmax_sub(b + 1, 1)
                    softmax_sub(b + 1, 2)
                else:
                    split_piece(6)
                power2(b, 1)

            power1(1)
            for i in range(3):
                softmax_sub(0, i)
            iteration(0, None, True)
            with pool.Fori(1, B - 1) as b:
                iteration(b, b - 1, True)
            iteration(B - 1, B - 2, False)
            split_piece(8)
            split_piece(10)
            split_piece(12)
            scatter_pairs(B - 1)
            split_piece(14)

            def gather(j, s, it):
                pool.wait_ge(ld_list[s], 16 * (it + 1))
                pass_waits(pool)
                nc.gpsimd.indirect_dma_start(
                    out=G[:, s, :], out_offset=None, in_=xrows[:, :],
                    in_offset=bass.IndirectOffsetOnAxis(ap=fresh[:, s, 0:1], axis=0)).then_inc(ld_rows[s], 16)

            def keep_entry(s):
                nc.gpsimd.tensor_copy(entry[:, s, :], fresh[:, s, :]).then_inc(entry_ready, 1)

            pool.wait_ge(st_rows, 16 * NT)
            for s in range(RING):
                gather(s, s, 0)
            keep_entry(0)
            keep_entry(1)
            pool.wait_ge(eT_mm, 1)
            gather(RING, 0, 1)
            pool.wait_ge(st_base, 16 * NT)

            def step(it, s, ahead=True, keep=True):
                j = RING * it + s
                before = (s + 2) % RING
                if not (isinstance(j, int) and j == 0):
                    pool.wait_ge(added[before], 16 * (it + (1 if s else 0)))
                    pass_waits(pool)
                if keep:
                    keep_entry(before)
                if ahead:
                    nxt = (s + 1) % RING
                    pool.wait_ge(eT_mm, j + 2)
                    gather(j + RING + 1, nxt, it + 1 + (s + 1) // RING)
                pool.wait_ge(entry_ready, j + 1)
                pool.wait_ge(ey_ready, j + 1)
                pass_waits(pool)
                nc.gpsimd.indirect_dma_start(
                    out=out, out_offset=bass.IndirectOffsetOnAxis(ap=entry[:, s, 0:1], axis=0),
                    in_=Y[:, s, :], in_offset=None, compute_op=ALU.add,
                    bounds_check=ROWS - 1, oob_is_err=True).then_inc(added[s], 16)

            for s in range(RING):
                step(0, s)
            with pool.Fori(1, ROUNDS - 2) as it:
                for s in range(RING):
                    step(it, s)
            for s in range(RING):
                step(ROUNDS - 2, s, ahead=s < 2)
            for s in range(RING):
                step(ROUNDS - 1, s, ahead=False, keep=s == 0)
            for s in range(RING):
                pool.wait_ge(added[s], 16 * ROUNDS)

        @block.scalar
        def _(act):
            def hi(dst, src, scale=1.0):
                return nc.scalar.activation(dst, src, ACT.Copy, scale=scale)

            def fill_k(b):
                for n in range(GH):
                    rows = slice(n * HD, (n + 1) * HD)
                    last = hi(kbdv[rows, :, :, n * SK:(n + 1) * SK],
                              kc[rows, :, :, bass.ds(b, 1), :].rearrange("p h g b k -> p h g (b k)"))
                    last.then_inc(k_filled, 1)

            def fill_v(b, parts):
                for d, n in (divmod(k, 2) for k in parts):
                    rows = slice(d * SK, (d + 1) * SK)
                    at = n * SK + d * HD
                    src = vc[rows, :, bass.ds(b, 1), :].rearrange("p h b (g n) -> p h (b g) n", g=NG)
                    dst = vbdv[rows, :, n::2, at:at + HD]
                    hi(dst, src[:, :, :, at:at + HD]).then_inc(v_filled, 1)

            act.wait_ge(ld_kv, 32)
            hi(ctx_s[:, 0].rearrange("p b e k -> p (b e k)"), ctx_raw, S_CTX).then_inc(kv_hi, 1)
            hi(wkv_s[:, 0, :], wkv_raw, S_W).then_inc(kv_hi, 1)
            act.wait_ge(ld_gates, 16)
            nc.scalar.activation(gl[:, 2:4], gl[:, 0:2], ACT.Tanh).then_inc(tanh_gates, 1)

            def norm1(b, i):
                t = 4 * b + i
                if isinstance(b, int):
                    act.wait_ge(ln1_stats, b + 1 if b < 2 else 3)
                else:
                    act.wait_ge(ln1_stats, 3)
                w = ln1[:, bass.ds(t, 1), :]
                nc.scalar.activation(xn1[:, i * D:(i + 1) * D], x_tile(t), ACT.Identity,
                                     bias=w[:, 0, 3:4], scale=w[:, 0, 2:3]).then_inc(xn1_ready, 1)

            for g in range(NG):
                act.wait_ge(k_mm, g + 1)
                hi(kc[:, 0, g].rearrange("p b k -> p (b k)"), mm_bank[g][:, 0:B * SK], S_KV / (S_CTX * S_W)).then_inc(k_hi, 1)
            act.wait_ge(ld_wq, 16)
            hi(wq_s[:, 0:DC * D], wq_raw, S_W).then_inc(wq_hi, 1)
            for i in range(PER):
                norm1(0, i)

            def values_hi(b):
                act.wait_ge(v_mm, b + 1)
                hi(vc[:, 0, b, :], mm_bank[b][:, :], S_KV / (S_CTX * S_W)).then_inc(v_hi, 1)

            def turn_hi(b, kind, i):
                number, bank_ = turn_no(b, kind, i)
                act.wait_ge(turned, number)
                turn_halves(lambda dst, src: hi(dst[0], src), kind, i, bank_).then_inc(turned_hi, 1)

            def scores_out(b, i):
                for h in range(2):
                    act.wait_ge(s_mm, 2 * (4 * b + i) + h + 1)
                    at = i * NH * SK + h * 512
                    nc.scalar.activation(S[:, at:at + 512], score_bank[h][:, :], ACT.Copy).then_inc(s_copied, 1)

            def exps(b, i):
                act.wait_ge(sub_ready, 4 * b + i + 1)
                si = S[:, i * NH * SK:(i + 1) * NH * SK]
                nc.scalar.activation(si, si, ACT.Exp, scale=float(HD) ** -0.5 / (S_Q * S_KV)).then_inc(exp_ready, 1)

            def tanh_h(b, i):
                act.wait_ge(h_mm, 4 * b + i + 1)
                nc.scalar.activation(th[:, i % 2, :], mm_bank[i % 2][:, 0:INTER], ACT.Tanh,
                                     scale=0.5 / (S_LN * S_W)).then_inc(th_ready, 1)

            def router_exp(b):
                act.wait_ge(lg_out, b + 1)
                nc.scalar.activation(ex[:, :, :], lg[:, :, :], ACT.Exp, scale=1.0 / (S_LN * S_W)).then_inc(lg_exp, 1)

            def split_piece(k):
                raw, whi, _ = w_piece(k)
                act.wait_ge(ld_w[w_slot(k)], 16 * w_round(k))
                if k in LO_BY_POOL:
                    hi(whi, raw, S_W)
                    hi(raw, raw, S_W).then_inc(w_hi, 1)
                else:
                    hi(whi, raw, S_W).then_inc(w_hi, 1)

            def feed_forward(f, soft, nxt, pieces):
                pieces = list(pieces)

                def split(n):
                    for _ in range(min(n, len(pieces))):
                        split_piece(pieces.pop(0))

                c = f + 1
                turn_hi(c, "x2", 0)
                if soft:
                    scores_out(c, 3)
                turn_hi(c, "x2", 1)
                if soft:
                    exps(c, 2)
                tanh_h(f, 0)
                if soft:
                    exps(c, 3)
                    tanh_h(f, 1)
                turn_hi(c, "x2", 2)
                turn_hi(c, "x2", 3)
                if not soft:
                    tanh_h(f, 1)
                    split(1)
                turn_hi(c, "g", 0)
                if nxt:
                    norm1(f + 2, 0)
                    norm1(f + 2, 1)
                if soft:
                    fill_v(c, (0, 1))
                split(1)
                tanh_h(f, 2)
                if soft:
                    fill_v(c, (2, 3))
                split(1)
                if nxt:
                    turn_hi(c, "x", 0)
                turn_hi(c, "g", 1)
                router_exp(f)
                if nxt:
                    norm1(f + 2, 2)
                    norm1(f + 2, 3)
                split(1)
                tanh_h(f, 3)
                if nxt:
                    fill_k(f + 2)
                for i in range(1, PER):
                    if nxt:
                        turn_hi(c, "x", i)
                    if i < 3:
                        turn_hi(c, "g", i + 1)
                split(len(pieces))

            def iteration(b, prev, nxt):
                if prev is None:
                    scores_out(b, 3)
                    fill_k(1)
                    for i in range(PER):
                        values_hi(i)
                        turn_hi(b, "x", i)
                        exps(b, i)
                    act.wait_ge(v_lo, B)
                    fill_v(0, range(4))
                else:
                    feed_forward(prev, True, nxt, () if nxt else range(2))
                for kind, n in mix(b):
                    if kind == "q":
                        project_hi(b + 1, n)
                        if prev is None:
                            if n == 2:
                                act.wait_ge(ld_shared, 32)
                            at = E * WE + (n - 2) * (HALF // 2)
                            if n >= 2:
                                hi(arena16[:, at:at + HALF // 2], shared_raw[n - 2], S_W).then_inc(shared_hi, 1)
                    else:
                        turn_hi(b, "p", 2 * n)
                        turn_hi(b, "p", 2 * n + 1)
                if not nxt:
                    split_piece(2)
                    split_piece(3)
                for g in range(NG):
                    act.wait_ge(a_mm, 4 * b + g + 1)
                    hi(aTv[:, 0, g, :], mm_bank[g][:, :], S_A / (S_P * S_KV)).then_inc(a_hi, 1)
                if nxt:
                    scores_out(b + 1, 0)
                    scores_out(b + 1, 1)
                    exps(b + 1, 0)
                    scores_out(b + 1, 2)
                    exps(b + 1, 1)
                else:
                    for k in range(4, 8):
                        split_piece(k)

            def project_hi(b, g):
                act.wait_ge(q_mm, 4 * b + g + 1)
                hi(qTv[:, 0, g, :], mm_bank[g][:, :], S_Q / (S_LN * S_W)).then_inc(q_hi, 1)

            for i in range(PER):
                turn_hi(None, "x", i)
            act.wait_ge(consts, CONSTS)
            act.wait_ge(k_lo, NG)
            fill_k(0)
            act.wait_ge(ld_wout, 16)
            hi(wout_s[:, 0:DC * D], wout_raw, S_W).then_inc(wout_hi, 1)
            for g in range(NG):
                project_hi(0, g)
                norm1(1, g)
            act.wait_ge(ld_gate, 16)
            hi(gate_s[:, 0].rearrange("p c e -> p (c e)"), gate_raw[:, :], S_W).then_inc(gate_hi, 1)
            act.wait_ge(wout_lo, 1)
            for i in range(3):
                scores_out(0, i)
            iteration(0, None, True)
            with act.Fori(1, B - 1) as b:
                iteration(b, b - 1, True)
            iteration(B - 1, B - 2, False)
            act.wait_ge(y_mm, NT)
            feed_forward(B - 1, False, False, range(8, PIECES))

            def rows_hi(j, s):
                act.wait_ge(eT_mm, j + 1)
                hi(GT[:, s, 0], e_turn[:, :].rearrange("p (c t) -> p c t", c=DC)).then_inc(eT_hi, 1)

            def tanh_e(j, s):
                act.wait_ge(eh_mm, j + 1)
                nc.scalar.activation(th[:, s, :], e_h[s][:, 0:INTER], ACT.Tanh,
                                     scale=0.5 / (S_LN * S_W)).then_inc(eth_ready, 1)

            def step(it, s, turn=True, nxt=True):
                j = RING * it + s
                if turn:
                    rows_hi(j + 2, (s + 2) % RING)
                act.wait_ge(egT_mm, j + 1)
                hi(gT[:, 0, 0], e_g[:, 0:IC * P].rearrange("p (c t) -> p c t", c=IC)).then_inc(egT_hi, 1)
                if nxt:
                    tanh_e(j + 1, (s + 1) % RING)
                act.wait_ge(ey_mm, j + 1)
                act.wait_ge(entry_ready, j + 1)
                if not isinstance(it, int) or it > 0:
                    act.wait_ge(added[s], 16 * it)
                nc.scalar.activation(Y[:, s, :], e_y[s][:, :], ACT.Copy,
                                     scale=entry[:, s, 1:2].bitcast(F32)).then_inc(ey_ready, 1)

            rows_hi(0, 0)
            rows_hi(1, 1)
            tanh_e(0, 0)
            for s in range(RING):
                step(0, s)
            with act.Fori(1, ROUNDS - 1) as it:
                for s in range(RING):
                    step(it, s)
            for s in range(RING):
                step(ROUNDS - 1, s, turn=s == 0, nxt=s < 2)

        @block.vector
        def _(dve):
            V = nc.vector

            def lo(dst, src, high, scale=1.0):
                if scale == 1.0:
                    return V.tensor_tensor(dst, src, high, ALU.subtract)
                return V.scalar_tensor_tensor(out=dst, in0=src, scalar=scale, in1=high, op0=ALU.mult, op1=ALU.subtract)

            dve.wait_ge(consts, CONSTS)
            V.tensor_scalar(empty[:, :, 0], empty[:, :, 0], P - 1, TOK, ALU.bitwise_and, ALU.bitwise_or).then_inc(zeroed, 1)
            dve.wait_ge(kv_hi, 2)
            lo(ctx_s[:, 1].rearrange("p b e k -> p (b e k)"), ctx_raw,
               ctx_s[:, 0].rearrange("p b e k -> p (b e k)"), S_CTX).then_inc(kv_lo, 1)
            lo(wkv_s[:, 1, :], wkv_raw, wkv_s[:, 0, :], S_W).then_inc(kv_lo, 1)

            def statistics(t, at, w, step_sem):
                return V.bn_stats(mv[:, at, 0:6], x_tile(t)).then_inc(step_sem, 1)

            def aggregate(at, w, n, step_sem, steps, var):
                dve.wait_ge(step_sem, steps)
                pass_waits(dve)
                for i in range(n):
                    ins = V.bn_aggr(w[:, i, 0:2], mv[:, at + i, 0:6])
                ins.then_inc(step_sem, 1)
                dve.wait_ge(step_sem, steps + 1)
                V.tensor_scalar(w[:, :, 1], w[:, :, 1], EPS, S_LN ** -2, ALU.add, ALU.mult).then_inc(var, 1)

            def prepare1(k):
                t0, t1 = LN1_GROUPS[k]
                w = ln1[:, t0:t1, :]
                for t in range(t0, t1):
                    statistics(t, t, w, ln1_step)
                aggregate(t0, w, t1 - t0, ln1_step, t1 + k, ln1_var)
                dve.wait_ge(ln1_power, k + 1)
                V.scalar_tensor_tensor(out=w[:, :, 3], in0=w[:, :, 0], scalar=-1.0, in1=w[:, :, 2],
                                       op0=ALU.mult, op1=ALU.mult).then_inc(ln1_stats, 1)

            def make_x1(b, i):
                t = 4 * b + i
                dve.wait_ge(y_mm, t + 1)
                V.scalar_tensor_tensor(out=x_tile(t), in0=mm_bank[i][:, :], scalar=gl[:, 0:1], in1=x_tile(t),
                                       op0=ALU.mult, op1=ALU.add).then_inc(x1_ready, 1)

            def statistics2(b, i):
                t = 4 * b + i
                dve.wait_ge(x1_ready, t + 1)
                pass_waits(dve)
                statistics(t, i, ln2, ln2_step)

            def x1_and_statistics(b, i):
                make_x1(b, i)
                statistics2(b, i)

            def aggregate2(b, p):
                aggregate(2 * p, ln2[:, 2 * p:2 * p + 2, :], 2, ln2_step, 6 * b + 3 * p + 2, ln2_var)

            def norm2(b, p):
                if not isinstance(b, int) or b > 0:
                    dve.wait_ge(st_rows, 64 * b)
                dve.wait_ge(ln2_power, 2 * b + p + 1)
                for i in (2 * p, 2 * p + 1):
                    V.tensor_scalar(xn2[:, i * D:(i + 1) * D], x_tile(4 * b + i), ln2[:, i, 0:1], ln2[:, i, 2:3],
                                    ALU.subtract, ALU.mult).then_inc(xn2_ready, 1)

            dve.wait_ge(ld_x0, 16)
            prepare1(0)
            dve.wait_ge(tanh_gates, 1)
            V.tensor_scalar(gl[:, 0:1], gl[:, 2:3], 1.0 / (S_A * S_W), None, ALU.mult).then_inc(gates_ready, 1)
            V.tensor_scalar(gl[:, 1:2], gl[:, 3:4], 1.0 / (S_G * S_W), None, ALU.mult).then_inc(gates_ready, 1)
            dve.wait_ge(gates_ready, 2)
            for g in range(NG):
                dve.wait_ge(k_hi, g + 1)
                lo(kc[:, 1, g].rearrange("p b k -> p (b k)"), mm_bank[g][:, 0:B * SK],
                   kc[:, 0, g].rearrange("p b k -> p (b k)"), S_KV / (S_CTX * S_W)).then_inc(k_lo, 1)
            dve.wait_ge(wq_hi, 1)
            lo(wq_s[:, DC * D:2 * DC * D], wq_raw, wq_s[:, 0:DC * D], S_W).then_inc(wq_lo, 1)

            def values_lo(b):
                dve.wait_ge(v_hi, b + 1)
                lo(vc[:, 1, b, :], mm_bank[b][:, :], vc[:, 0, b, :], S_KV / (S_CTX * S_W)).then_inc(v_lo, 1)

            def turn_lo(b, kind, i):
                number, bank_ = turn_no(b, kind, i)
                dve.wait_ge(turned_hi, number)
                turn_halves(lambda dst, src: lo(dst[1], src, dst[0]), kind, i, bank_).then_inc(turned_lo, 1)

            def head_max(b, i):
                if i == 0:
                    dve.wait_ge(masked, b + 1)
                else:
                    dve.wait_ge(s_copied, 2 * (4 * b + i) + 2)
                V.tensor_reduce(mx[:, i, :], S[:, i * NH * SK:(i + 1) * NH * SK].rearrange("p (h k) -> p h k", h=NH),
                                AX.X, ALU.max).then_inc(max_ready, 1)

            def head_sum(b, i):
                t = 4 * b + i
                dve.wait_ge(exp_ready, t + 1)
                V.tensor_reduce(mx[:, i, :], S[:, i * NH * SK:(i + 1) * NH * SK].rearrange("p (h k) -> p h k", h=NH),
                                AX.X, ALU.add).then_inc(sum_ready, 1)
                dve.wait_ge(sum_ready, 2 * t + 1)
                V.tensor_scalar(mx[:, i, :], mx[:, i, :], 1.0 / S_P, None, ALU.mult).then_inc(sum_ready, 1)
                dve.wait_ge(sum_ready, 2 * t + 2)
                V.reciprocal(rd[:, i, :], mx[:, i, :]).then_inc(rd_ready, 1)

            def over(v):
                return v.unsqueeze(2).to_broadcast([P, PER, E])

            def each_tile(v):
                return v.unsqueeze(1).to_broadcast([P, PER, E])

            lg_bank = mm_bank[3][:, 0:PER * E].rearrange("p (i e) -> p i e", i=PER)

            def router_logits(b):
                dve.wait_ge(lg_mm, b + 1)
                V.tensor_reduce(m[:, 0, :], lg_bank, AX.X, ALU.max).then_inc(lg_max, 1)
                dve.wait_ge(lg_max, b + 1)
                V.tensor_tensor(lg[:, :, :], lg_bank, over(m[:, 0, :]), ALU.subtract).then_inc(lg_out, 1)

            ROUTE = 13

            def router_choose(b, k):
                n = [9 * k]

                def link(ins):
                    n[0] += 1
                    ins.then_inc(route_step, 1)
                    dve.wait_ge(route_step, ROUTE * b + n[0])

                if k == 0:
                    dve.wait_ge(lg_exp, b + 1)
                    link(V.tensor_reduce(m[:, 1, :], ex[:, :, :], AX.X, ALU.add))
                    link(V.reciprocal(m[:, 2, :], m[:, 1, :]))
                    link(V.tensor_tensor(sc[:, :, :], ex[:, :, :], over(m[:, 2, :]), ALU.mult))
                src = sc2 if k else sc
                link(V.tensor_reduce(m[:, 3 + k, :], src[:, :, :], AX.X, ALU.max))
                link(V.tensor_tensor(eq[:, :, :], src[:, :, :], over(m[:, 3 + k, :]), ALU.is_equal))
                link(V.tensor_tensor(eq[:, :, :], eq[:, :, :], each_tile(first_high[:, :]), ALU.mult))
                link(V.tensor_reduce(m[:, 5, :], eq[:, :, :], AX.X, ALU.max))
                if k == 0:
                    link(V.tensor_tensor(oh[:, 0], eq[:, :, :], over(m[:, 5, :]), ALU.is_equal))
                    link(V.scalar_tensor_tensor(out=sc2[:, :, :], in0=oh[:, 0], scalar=-2.0, in1=sc[:, :, :],
                                                op0=ALU.mult, op1=ALU.add))
                    assert n[0] == 9
                    return
                assert n[0] == ROUTE
                ins = V.tensor_tensor(oh[:, 1], eq[:, :, :], over(m[:, 5, :]), ALU.is_equal)
                ins.then_inc(route2_step, 1)
                dve.wait_ge(route2_step, ROUTE2 * b + 1)
                V.tensor_tensor(mask16[:, :].rearrange("p (i e) -> p i e", i=PER), oh[:, 0], oh[:, 1],
                                ALU.add).then_inc(mask_ready, 1)

            ROUTE2 = 9

            def router_place(b):
                n = [1]

                def link(ins):
                    n[0] += 1
                    ins.then_inc(route2_step, 1)
                    dve.wait_ge(route2_step, ROUTE2 * b + n[0])

                dve.wait_ge(pos_mm, b + 1)
                link(V.tensor_tensor(pos[:, :, :], score_bank[0][:, 0:PER * E].rearrange("p (i e) -> p i e", i=PER),
                                     each_tile(seen[:, :]), ALU.add))
                V.tensor_tensor(seen[:, :], score_bank[0][:, PER * E:PER * E + E], seen[:, :], ALU.add).then_inc(pos_out, 1)
                if not isinstance(b, int) or b > 0:
                    dve.wait_ge(st_pairs, 16 * 2 * PER * b)
                for k in range(2):
                    link(V.tensor_tensor(sel[:, :, :], pos[:, :, :], oh[:, k], ALU.mult))
                    link(V.tensor_reduce(slot[:, :, k], sel[:, :, :], AX.X, ALU.add))
                    link(V.tensor_scalar(pair[:, :, k, 1].bitcast(F32), m[:, 3 + k, :], gl[:, 1:2], None, ALU.mult))
                link(V.tensor_scalar(pair[:, :, :, 0], pair[:, :, :, 0], float(SQ), None, ALU.add))
                assert n[0] == ROUTE2
                V.tensor_copy(count[:, 0, :], seen[:, :]).then_inc(pairs_ready, 1)

            def hidden(b, i):
                t = 4 * b + i
                s = i % 2
                dve.wait_ge(th_ready, t + 1)
                V.scalar_tensor_tensor(out=uu[:, s, :], in0=th[:, s, :], scalar=1.0, in1=mm_bank[s][:, 0:INTER],
                                       op0=ALU.add, op1=ALU.mult).then_inc(u_ready, 1)
                dve.wait_ge(u_ready, t + 1)
                V.scalar_tensor_tensor(out=gg[:, s, :], in0=uu[:, s, :], scalar=0.5 * S_G / (S_LN * S_W) ** 2,
                                       in1=mm_bank[s][:, INTER:2 * INTER], op0=ALU.mult,
                                       op1=ALU.mult).then_inc(g_ready, 1)

            def base(b, i):
                t = 4 * b + i
                dve.wait_ge(z_mm, t + 1)
                V.scalar_tensor_tensor(out=x_tile(t), in0=mm_bank[2 + i % 2][:, :], scalar=gl[:, 1:2],
                                       in1=x_tile(t), op0=ALU.mult, op1=ALU.add).then_inc(base_ready, 1)

            def split_piece(k):
                raw, whi, wlo = w_piece(k)
                dve.wait_ge(w_hi, k + 1)
                lo(wlo, raw, whi, S_W).then_inc(w_split[w_slot(k)], 1)

            def after_attention(f):
                c = f + 1
                turn_lo(c, "x2", 0)
                statistics2(f, 3)
                aggregate2(f, 1)
                turn_lo(c, "x2", 1)
                norm2(f, 1)

            def feed_forward(f, nxt):
                c = f + 1
                after_attention(f)
                head_max(c, 3)
                hidden(f, 0)
                turn_lo(c, "x2", 2)
                turn_lo(c, "x2", 3)
                hidden(f, 1)
                turn_lo(c, "g", 0)
                head_sum(c, 0)
                head_sum(c, 1)
                hidden(f, 2)
                if nxt:
                    turn_lo(c, "x", 0)
                turn_lo(c, "g", 1)
                router_logits(f)
                base(f, 0)
                router_choose(f, 0)
                hidden(f, 3)
                if nxt:
                    turn_lo(c, "x", 1)
                turn_lo(c, "g", 2)
                router_choose(f, 1)
                if nxt:
                    turn_lo(c, "x", 2)
                turn_lo(c, "g", 3)
                base(f, 1)
                base(f, 2)
                head_sum(c, 2)
                if nxt:
                    turn_lo(c, "x", 3)
                router_place(f)
                base(f, 3)
                head_sum(c, 3)

            def last_feed_forward(f):
                c = f + 1
                after_attention(f)
                hidden(f, 0)
                turn_lo(c, "x2", 2)
                turn_lo(c, "x2", 3)
                hidden(f, 1)
                split_piece(9)
                turn_lo(c, "g", 0)
                router_logits(f)
                router_choose(f, 0)
                router_choose(f, 1)
                hidden(f, 2)
                turn_lo(c, "g", 1)
                base(f, 0)
                router_place(f)
                hidden(f, 3)
                base(f, 1)
                turn_lo(c, "g", 2)
                split_piece(11)
                turn_lo(c, "g", 3)
                base(f, 2)
                base(f, 3)

            def project_lo(b, g):
                dve.wait_ge(q_hi, 4 * b + g + 1)
                lo(qTv[:, 1, g, :], mm_bank[g][:, :], qTv[:, 0, g, :], S_Q / (S_LN * S_W)).then_inc(q_lo, 1)

            def iteration(b, prev, nxt):
                if prev is None:
                    head_max(b, 3)
                    for i in range(PER):
                        values_lo(i)
                        turn_lo(b, "x", i)
                        head_sum(b, i)
                    dve.wait_ge(ld_x, 16)
                    prepare1(2)
                else:
                    feed_forward(prev, nxt)
                for kind, n in mix(b):
                    if kind == "q":
                        project_lo(b + 1, n)
                        if prev is None and n >= 2:
                            at = E * WE + (n - 2) * (HALF // 2)
                            dve.wait_ge(shared_hi, n - 1)
                            lo(arena16[:, at + HALF:at + HALF + HALF // 2], shared_raw[n - 2],
                               arena16[:, at:at + HALF // 2], S_W).then_inc(shared_lo, 1)
                    else:
                        turn_lo(b, "p", 2 * n)
                        turn_lo(b, "p", 2 * n + 1)
                if not nxt:
                    split_piece(2)
                    split_piece(3)
                for g in range(NG):
                    dve.wait_ge(a_hi, 4 * b + g + 1)
                    lo(aTv[:, 1, g, :], mm_bank[g][:, :], aTv[:, 0, g, :], S_A / (S_P * S_KV)).then_inc(a_lo, 1)
                x1_and_statistics(b, 0)
                if nxt:
                    head_max(b + 1, 0)
                    head_max(b + 1, 1)
                else:
                    split_piece(5)
                x1_and_statistics(b, 1)
                aggregate2(b, 0)
                norm2(b, 0)
                if nxt:
                    head_max(b + 1, 2)
                else:
                    split_piece(7)
                x1_and_statistics(b, 2)
                make_x1(b, 3)

            for i in range(PER):
                turn_lo(None, "x", i)
            dve.wait_ge(ld_x1, 16)
            prepare1(1)
            project_lo(0, 0)
            dve.wait_ge(wout_hi, 1)
            lo(wout_s[:, DC * D:2 * DC * D], wout_raw, wout_s[:, 0:DC * D], S_W).then_inc(wout_lo, 1)
            for g in range(1, NG):
                project_lo(0, g)
            dve.wait_ge(gate_hi, 1)
            lo(gate_s[:, 1].rearrange("p c e -> p (c e)"), gate_raw[:, :],
               gate_s[:, 0].rearrange("p c e -> p (c e)"), S_W).then_inc(gate_lo, 1)
            for i in range(3):
                head_max(0, i)
            iteration(0, None, True)
            with dve.Fori(1, B - 1) as b:
                iteration(b, b - 1, True)
            iteration(B - 1, B - 2, False)
            last_feed_forward(B - 1)

            n = [0]

            def link(ins):
                n[0] += 1
                ins.then_inc(table_step, 1)
                dve.wait_ge(table_step, n[0])

            r = slice(0, 1)

            def by_tile(v):
                return v.unsqueeze(1).to_broadcast([1, TILES, E])

            dve.wait_ge(pairs_ready, B)
            link(V.tensor_tensor(count[r, 1, :], count[r, 0, :], list_at[r, :], ALU.subtract))
            link(V.tensor_scalar(count_i[r, 0, :], count[r, 1, :], float(P - 1), None, ALU.add))
            link(V.tensor_scalar(count_i[r, 1, :], count_i[r, 0, :], 7, None, ALU.arith_shift_right))
            link(V.tensor_copy(count[r, 2, :], count_i[r, 1, :]))
            link(V.memset(count[r, 3, :], 1.0))
            link(V.tensor_tensor_scan(count[r, 4, :], count[r, 3, :], count[r, 2, :], 0.0, ALU.mult, ALU.add))
            link(V.tensor_scalar(count[r, 5, :], count[r, 2, :], -float(P), float(LIST), ALU.mult, ALU.add))
            link(V.tensor_tensor(past[r], tile_no[r, :].unsqueeze(2).to_broadcast([1, TILES, E]),
                                 by_tile(count[r, 4, :]), ALU.is_ge))
            link(V.tensor_reduce(tab[r, 0, :], past[r], AX.X, ALU.add))
            link(V.tensor_tensor(skip[r], past[r], by_tile(count[r, 5, :]), ALU.mult))
            link(V.tensor_reduce(tab_f[r, 0, :], skip[r], AX.X, ALU.add))
            link(V.scalar_tensor_tensor(out=tab_f[r, 1, :], in0=tile_no[r, :], scalar=float(P), in1=tab_f[r, 0, :],
                                        op0=ALU.mult, op1=ALU.add))
            V.tensor_copy(tab[r, 1, :], tab_f[r, 1, :]).then_inc(table_ready, 1)
            split_piece(13)
            split_piece(15)

            def rows_lo(j, s):
                dve.wait_ge(eT_hi, j + 1)
                lo(GT[:, s, 1], e_turn[:, :].rearrange("p (c t) -> p c t", c=DC), GT[:, s, 0]).then_inc(eT_lo, 1)

            def hidden_e(j, s):
                dve.wait_ge(eth_ready, j + 1)
                V.scalar_tensor_tensor(out=uu[:, s, :], in0=th[:, s, :], scalar=1.0, in1=e_h[s][:, 0:INTER],
                                       op0=ALU.add, op1=ALU.mult).then_inc(eu_ready, 1)
                dve.wait_ge(eu_ready, j + 1)
                V.scalar_tensor_tensor(out=gg[:, s, :], in0=uu[:, s, :], scalar=0.5 * S_G / (S_LN * S_W) ** 2,
                                       in1=e_h[s][:, INTER:2 * INTER], op0=ALU.mult,
                                       op1=ALU.mult).then_inc(eg_ready, 1)

            def step(it, s, turn=True, nxt=True):
                j = RING * it + s
                if turn:
                    rows_lo(j + 2, (s + 2) % RING)
                dve.wait_ge(egT_hi, j + 1)
                lo(gT[:, 0, 1], e_g[:, 0:IC * P].rearrange("p (c t) -> p c t", c=IC), gT[:, 0, 0]).then_inc(egT_lo, 1)
                if nxt:
                    hidden_e(j + 1, (s + 1) % RING)

            rows_lo(0, 0)
            rows_lo(1, 1)
            hidden_e(0, 0)
            for s in range(RING):
                step(0, s)
            with dve.Fori(1, ROUNDS - 1) as it:
                for s in range(RING):
                    step(it, s)
            for s in range(RING):
                step(ROUNDS - 1, s, turn=s == 0, nxt=s < 2)

        @block.tensor
        def _(pe):
            def product(dst, pairs):
                steps = [(a(u), b(v)) for a, b in pairs for u, v in ((0, 0), (0, 1), (1, 0))]
                for n, (a, b) in enumerate(steps):
                    last = nc.tensor.matmul(dst, a, b, start=n == 0, stop=n == len(steps) - 1)
                return last

            def turn(dst, src, n):
                for c in range(n):
                    last = nc.tensor.transpose(dst[:, c * P:(c + 1) * P], src[:, c * P:(c + 1) * P], ident[:, :])
                return last

            pe.wait_ge(consts, 5)
            pe.wait_ge(kv_lo, 2)
            for g in range(NG):
                product(mm_bank[g][:, 0:B * SK].rearrange("p (b k) -> p b k", b=B),
                        [(lambda h, g=g: wkv_s[:, h, g * P:(g + 1) * P],
                          lambda h: ctx_s[:, h, :, 0, :])]).then_inc(k_mm, 1)
            def values(b):
                pe.wait_ge(q_lo, b + 1)
                product(mm_bank[b][:, :],
                        [(lambda h, b=b: ctx_s[:, h, b].rearrange("p e k -> p (e k)"),
                          lambda h: wkv_s[:, h, D:2 * D])]).then_inc(v_mm, 1)

            def router(i0, i1):
                for i in range(i0, i1):
                    cols = mm_bank[3][:, i * E:(i + 1) * E]
                    last = product(cols, [(lambda h, c=c, i=i: x2T[:, h, c, i * P:(i + 1) * P],
                                           lambda h, c=c: gate_s[:, h, c, :]) for c in range(DC)])
                return last

            def shared_w(h, c):
                at = E * WE + h * HALF + c * D
                return arena16[:, at:at + D]

            def turn_tile(b, kind, i):
                number, bank_ = turn_no(b, kind, i)
                if not (b is None and i < 2):
                    pe.wait_ge(turned_lo, number - 2)
                src = {"x": xn1, "x2": xn2, "p": S, "g": gg[:, i % 2, :]}[kind]
                n = IC if kind == "g" else DC
                if kind != "g":
                    src = src[:, i * D:(i + 1) * D]
                turn(bank_, src, n).then_inc(turned, 1)

            def split_done(b, kind, i):
                pe.wait_ge(turned_lo, turn_no(b, kind, i)[0])

            def hidden(f, i):
                split_done(f + 1, "x2", i)
                if i >= 2:
                    pe.wait_ge(g_ready, 4 * f + i - 1)
                product(mm_bank[i % 2][:, :], [(lambda h, c=c: x2T[:, h, c, i * P:(i + 1) * P],
                                                lambda h, c=c: shared_w(h, c)) for c in range(DC)]).then_inc(h_mm, 1)

            def turn_g(f, i):
                pe.wait_ge(g_ready, 4 * f + i + 1)
                turn_tile(f + 1, "g", i)

            def down(f, i):
                split_done(f + 1, "g", i)
                if i == 1:
                    pe.wait_ge(lg_out, f + 1)
                if i >= 2:
                    pe.wait_ge(base_ready, 4 * f + i - 1)
                product(mm_bank[2 + i % 2][:, :], [(lambda h, c=c: gT[:, i % 2, h, c, :],
                                                    lambda h, c=c: shared_w(h, DC + c))
                                                   for c in range(IC)]).then_inc(z_mm, 1)

            def count_pairs(f):
                pe.wait_ge(mask_ready, f + 1)
                if not isinstance(f, int) or f < B - 1:
                    pe.wait_ge(s_copied, 8 * f + 16)
                dst = score_bank[0]
                nc.tensor.matmul(dst[:, 0:PER * E], earlier[:, :], mask16[:, :], start=True, stop=False)
                for i in range(1, PER):
                    nc.tensor.matmul(dst[:, i * E:PER * E], ones16[:, :], mask16[:, 0:(PER - i) * E],
                                     start=False, stop=i == PER - 1)
                for i in range(PER):
                    last = nc.tensor.matmul(dst[:, PER * E:PER * E + E], ones16[:, :], mask16[:, i * E:(i + 1) * E],
                                            start=i == 0, stop=i == PER - 1)
                last.then_inc(pos_mm, 1)

            def turn_x(b, i):
                pe.wait_ge(xn1_ready, (0 if b is None else 4 * b + 4) + i + 1)
                turn_tile(b, "x", i)

            def turn_x2(f, i):
                pe.wait_ge(xn2_ready, 4 * f + i + 1)
                turn_tile(f + 1, "x2", i)

            def scores(b, i):
                for half in range(2):
                    if not (isinstance(b, int) and b == 0 and i == 0):
                        pe.wait_ge(s_copied, 2 * (4 * b + i) + half - 1)
                    for g in (2 * half, 2 * half + 1):
                        last = product(score_bank[half][:, (g % 2) * 256:(g % 2 + 1) * 256],
                                       [(lambda h: qTv[:, h, g, i * P:(i + 1) * P], lambda h: kbdv[:, h, g, :])])
                    last.then_inc(s_mm, 1)

            def project(b, g):
                product(mm_bank[g][:, :], [(lambda h, c=c: wqv[:, h, c, g * P:(g + 1) * P],
                                            lambda h, c=c: xTv[:, h, c, :]) for c in range(DC)]).then_inc(q_mm, 1)

            def feed_forward(f, nxt):
                c = f + 1
                turn_x2(f, 0)
                scores(c, 3)
                turn_x2(f, 1)
                hidden(f, 0)
                hidden(f, 1)
                turn_x2(f, 2)
                turn_x2(f, 3)
                turn_g(f, 0)
                router(0, 2)
                hidden(f, 2)
                split_done(c, "x2", 3)
                router(2, 4).then_inc(lg_mm, 1)
                if nxt:
                    turn_x(c, 0)
                turn_g(f, 1)
                down(f, 0)
                hidden(f, 3)
                if nxt:
                    turn_x(c, 1)
                turn_g(f, 2)
                down(f, 1)
                if nxt:
                    turn_x(c, 2)
                turn_g(f, 3)
                down(f, 2)
                if nxt:
                    turn_x(c, 3)
                count_pairs(f)
                down(f, 3)

            def last_feed_forward(f):
                turn_x2(f, 0)
                turn_x2(f, 1)
                hidden(f, 0)
                turn_x2(f, 2)
                turn_x2(f, 3)
                hidden(f, 1)
                split_done(f + 1, "x2", 3)
                router(0, 4).then_inc(lg_mm, 1)
                turn_g(f, 0)
                hidden(f, 2)
                turn_g(f, 1)
                down(f, 0)
                count_pairs(f)
                hidden(f, 3)
                down(f, 1)
                turn_g(f, 2)
                turn_g(f, 3)
                down(f, 2)
                down(f, 3)

            def iteration(b, prev, nxt):
                if prev is None:
                    scores(b, 3)
                    for i in range(PER):
                        values(i)
                        turn_x(b, i)
                else:
                    feed_forward(prev, nxt)
                for kind, n in mix(b):
                    if kind == "q":
                        if n == 0:
                            split_done(b, "x", 3)
                        if prev is None:
                            pe.wait_ge(v_lo, n + 1)
                        elif n >= 2:
                            pe.wait_ge(base_ready, 4 * b + n - 3)
                        project(b + 1, n)
                    else:
                        pe.wait_ge(p_ready, 4 * b + n + 1)
                        turn_tile(b, "p", 2 * n)
                        turn_tile(b, "p", 2 * n + 1)
                split_done(b, "p", 2 * PER - 1)
                pe.wait_ge(v_filled, 4 * (b + 1))
                if not nxt:
                    pe.wait_ge(base_ready, 4 * b)
                for g in range(NG):
                    if nxt:
                        pe.wait_ge(q_lo, 4 * (b + 1) + g + 1)
                    product(mm_bank[g][:, :], [(lambda h, r=r: vbdv[:, h, r, :], lambda h, r=r: PTv[:, h, r, :])
                                               for r in (2 * g, 2 * g + 1)]).then_inc(a_mm, 1)
                if nxt:
                    pe.wait_ge(k_filled, GH * (b + 2))
                    if prev is not None:
                        pe.wait_ge(pos_out, b)
                    scores(b + 1, 0)
                pe.wait_ge(a_lo, 4 * b + 4)
                if prev is None:
                    pe.wait_ge(wout_lo, 1)
                for i in range(PER):
                    product(mm_bank[i][:, :], [(lambda h, g=g: aTv[:, h, g, i * P:(i + 1) * P],
                                                lambda h, g=g: woutv[:, h, g, :]) for g in range(NG)]).then_inc(y_mm, 1)
                    if nxt and i < 2:
                        scores(b + 1, i + 1)

            for i in range(PER):
                turn_x(None, i)
            pe.wait_ge(wq_lo, 1)
            split_done(None, "x", 3)
            for g in range(NG):
                pe.wait_ge(k_lo, g + 1)
                project(0, g)
            pe.wait_ge(q_lo, 4)
            pe.wait_ge(k_filled, GH)
            for i in range(3):
                scores(0, i)
            iteration(0, None, True)
            pe.wait_ge(gate_lo, 1)
            pe.wait_ge(shared_lo, 2)
            with pe.Fori(1, B - 1) as b:
                iteration(b, b - 1, True)
            iteration(B - 1, B - 2, False)
            last_feed_forward(B - 1)

            def expert_of(j):
                return nc.values_load(tab[0:1, 0, bass.ds(j, 1)], engines=[PE_ENGINE], min_val=0, max_val=E,
                                      skip_runtime_bounds_check_because="a count of experts passed, at most E")

            def w_at(e, h, c):
                return arena16[:, bass.ds(e * WE + (h * HALF + c * D), D)]

            def turn_rows(j, s, it):
                pe.wait_ge(ld_rows[s], 16 * (it + 1))
                if not isinstance(j, int) or j > 0:
                    pe.wait_ge(eT_lo, j)
                turn(e_turn, G[:, s, :], DC).then_inc(eT_mm, 1)

            def hidden_e(j, s):
                e = expert_of(j)
                pe.wait_ge(eT_lo, j + 1)
                product(e_h[s][:, :], [(lambda h, c=c: GT[:, s, h, c, :], lambda h, c=c: w_at(e, h, c))
                                       for c in range(DC)]).then_inc(eh_mm, 1)

            def step(it, s, turn_=True, nxt=True):
                j = RING * it + s
                if turn_:
                    turn_rows(j + 2, (s + 2) % RING, it + (s + 2) // RING)
                pe.wait_ge(eg_ready, j + 1)
                if not isinstance(j, int) or j > 0:
                    pe.wait_ge(egT_lo, j)
                turn(e_g, gg[:, s, :], IC).then_inc(egT_mm, 1)
                if nxt:
                    hidden_e(j + 1, (s + 1) % RING)
                e = expert_of(j)
                pe.wait_ge(egT_lo, j + 1)
                if not isinstance(it, int) or it > 0:
                    pe.wait_ge(ey_ready, j - 2)
                product(e_y[s][:, :], [(lambda h, c=c: gT[:, 0, h, c, :], lambda h, c=c: w_at(e, h, DC + c))
                                       for c in range(IC)]).then_inc(ey_mm, 1)

            pe.wait_ge(base_ready, NT)
            pe.wait_ge(pos_out, B)
            pe.wait_ge(table_ready, 1)
            turn_rows(0, 0, 0)
            turn_rows(1, 1, 0)
            for k in range(PIECES - 4, PIECES):
                pe.wait_ge(w_split[w_slot(k)], w_round(k))
            hidden_e(0, 0)
            for s in range(RING):
                step(0, s)
            with pe.Fori(1, ROUNDS - 1) as it:
                for s in range(RING):
                    step(it, s)
            for s in range(RING):
                step(ROUNDS - 1, s, turn_=s == 0, nxt=s < 2)


def kernel(**inputs):
    import concourse.bacc as bacc
    from concourse.bass_utils import run_bass_kernel_spmd

    v = {n: np.asarray(a) for n, a in inputs.items()}

    def chunks(w):
        return w.reshape(-1, P, w.shape[1]).transpose(1, 0, 2).reshape(P, -1)

    def expert(w1, w2, w3):
        up = np.concatenate([w1.T, w3.T], axis=1)
        return np.concatenate([chunks(up), chunks(w2.T)], axis=1)

    ctx_t = v["ctx_512"].transpose(2, 0, 1)
    arrays = {
        "x": v["x"].reshape(NT, P, D).transpose(1, 0, 2),
        "ctx_rows": np.stack([ctx_t, ctx_t], axis=2),
        "gates": np.broadcast_to(np.concatenate([v["g_xattn"], v["g_ffn"]])[None, :], (P, 2)),
        "wq": chunks(v["L0_xattn_Wq"].T),
        "wkv": v["L0_xattn_Wkv_expand"].T,
        "wout": chunks(v["L0_xattn_Wout"].T),
        "gate_w": chunks(v["L0_ffn_gate_w"].T),
        "experts": np.stack([expert(v["L0_ffn_w1"][e], v["L0_ffn_w2"][e], v["L0_ffn_w3"][e]) for e in range(E)]
                            + [expert(v["L0_ffn_ws1"], v["L0_ffn_ws2"], v["L0_ffn_ws3"])]),
    }
    arrays = {n: np.ascontiguousarray(a) for n, a in arrays.items()}
    nc = bacc.Bacc("TRN2", target_bir_lowering=False, num_devices=1)
    args = [nc.dram_tensor("in_" + n, a.shape, mybir.dt.from_np(a.dtype), kind="ExternalInput").ap()
            for n, a in arrays.items()]
    out = nc.dram_tensor("out", (ROWS, D), F32, kind="ExternalOutput").ap()
    block_program(nc, *args, out)
    r = run_bass_kernel_spmd(nc, [{"in_" + n: a for n, a in arrays.items()}], core_ids=[0])
    return r.results[0]["out"][:TOK].reshape(B, SQ, D)
```
